# Optimizing a Trainium2 kernel written in Bass

```python
import numpy as np
import jax
import jax.numpy as jnp

def _softmax(x, axis=-1):
    return jax.nn.softmax(x, axis=axis)

def _gelu(x):
    return jax.nn.gelu(x, approximate=True)

def _silu(x):
    return jax.nn.silu(x)

def _sigmoid(x):
    return jax.nn.sigmoid(x)

def _layernorm(x, axis=-1, eps=1e-05):
    m = jnp.mean(x, axis=axis, keepdims=True)
    v = jnp.var(x, axis=axis, keepdims=True)
    return (x - m) / jnp.sqrt(v + eps)

def _scatter_add(tgt, idx, src, axis=0):
    return tgt.at[idx].add(src)

def _segment_sum(src, seg, n):
    return jax.ops.segment_sum(src, seg, n)
kernel_name = 'mk_decoder_preln_d1_seqx_r8_584341'

def setup_inputs(seed: int=0):
    np.random.seed(seed)
    _w = jnp.asarray

    def _rec_inputs():
        import jax
        import jax.numpy as jnp
        _rk = jax.random.key(seed)
        x = -0.000125 + 0.9999 * jax.random.normal(jax.random.fold_in(_rk, 1), (4, 256, 256), jnp.float32)
        _lenS = 256 - jax.random.randint(jax.random.fold_in(_rk, 7), (4,), 0, max(1, 256 // 4) + 1, jnp.int32)
        _lenS2 = 256 - jax.random.randint(jax.random.fold_in(_rk, 8), (4,), 0, max(1, 256 // 4) + 1, jnp.int32)
        itok_BxS_13_99985 = jax.random.randint(jax.random.fold_in(_rk, 11), (4, 256), 13, 99986, jnp.int32)
        _ctx_2048P = jax.random.normal(jax.random.fold_in(_rk, 12), (4, 16, 256), jnp.float32)
        _ctx_2048c = jax.random.dirichlet(jax.random.fold_in(_rk, 512), 0.3 * jnp.ones((16,), jnp.float32), (4, 256))
        _ctx_2048t = jnp.einsum('bsk,bkd->bsd', _ctx_2048c, _ctx_2048P)
        _ctx_2048t = _ctx_2048t * jax.lax.rsqrt(jnp.mean(jnp.square(_ctx_2048t)) + 1e-12) * 0.953939
        ctx_2048 = 6.82029e-06 + 0.0200006 * (_ctx_2048t + 0.3 * jax.random.normal(jax.random.fold_in(_rk, 612), (4, 256, 256), jnp.float32))
        return (x, itok_BxS_13_99985, ctx_2048)
    x, itok_BxS_13_99985, ctx_2048 = _rec_inputs()

    def _L0_attn_setup():
        import jax, jax.numpy as jnp
        import numpy as np
        HIDDEN = 256
        KEY = 256
        EPS = 1e-05
        key = jax.random.key(seed)
        k1, k2, k3 = jax.random.split(key, 3)
        B, S = (4, 256)
        x = jax.random.normal(k1, (B, S, HIDDEN), dtype=jnp.float32)
        bq = 1.0 / np.sqrt(HIDDEN)
        qkv = jax.random.uniform(k2, (HIDDEN, KEY * 3), minval=-bq, maxval=bq, dtype=jnp.float32)
        bo = 1.0 / np.sqrt(KEY)
        o_proj = jax.random.uniform(k3, (KEY, HIDDEN), minval=-bo, maxval=bo, dtype=jnp.float32)
        gamma = jnp.ones((HIDDEN,), dtype=jnp.float32)
        beta = jnp.zeros((HIDDEN,), dtype=jnp.float32)
        return {'x': x, 'qkv': qkv, 'o_proj': o_proj, 'gamma': gamma, 'beta': beta}
    _L0_attn_all = _L0_attn_setup()
    _L0_attn_in = {k: v for k, v in _L0_attn_all.items() if k in ('qkv', 'o_proj', 'gamma', 'beta')}
    del _L0_attn_all

    def _L0_xattn_setup():
        import jax, jax.numpy as jnp
        import numpy as np
        B, S, D = (4, 512, 256)
        E = 4
        F = 1024 // E
        VOCAB = 12500
        key = jax.random.key(seed)
        k1, k2, k3, k4, k5 = jax.random.split(key, 5)
        hidden_states = jax.random.normal(k1, (B, S, D), dtype=jnp.float32)
        token_ids = jax.random.randint(k2, (B, S), 0, VOCAB, dtype=jnp.int64)
        Wg = jax.random.normal(k3, (E, F, D), dtype=jnp.float32) * 0.02
        Wu = jax.random.normal(k4, (E, F, D), dtype=jnp.float32) * 0.02
        Wd = jax.random.normal(k5, (E, D, F), dtype=jnp.float32) * 0.02
        return {'hidden_states': hidden_states, 'token_ids': token_ids, 'Wg': Wg, 'Wu': Wu, 'Wd': Wd}
    _L0_xattn_all = _L0_xattn_setup()
    _L0_xattn_in = {k: v for k, v in _L0_xattn_all.items() if k in ()}
    del _L0_xattn_all

    def _L0_ffn_setup():
        import jax, jax.numpy as jnp
        import numpy as np
        NUM_EXPERTS = 12
        TOP_K = 2
        FFN_DIM = 160
        HIDDEN = 256
        key = jax.random.key(seed)
        k0, k1, k2, k3, k4 = jax.random.split(key, 5)
        B, S, H, F, E = (4, 128, HIDDEN, FFN_DIM, NUM_EXPERTS)
        hidden_states = jax.random.normal(k0, (B, S, H), dtype=jnp.float32)
        gate_w = jax.random.normal(k1, (E, H), dtype=jnp.float32) * 0.02
        w1 = jax.random.normal(k2, (E, F, H), dtype=jnp.float32) * 0.02
        w2 = jax.random.normal(k3, (E, H, F), dtype=jnp.float32) * 0.02
        w3 = jax.random.normal(k4, (E, F, H), dtype=jnp.float32) * 0.02
        return {'hidden_states': hidden_states, 'gate_w': gate_w, 'w1': w1, 'w2': w2, 'w3': w3}
    _L0_ffn_all = _L0_ffn_setup()
    _L0_ffn_in = {k: v for k, v in _L0_ffn_all.items() if k in ('gate_w', 'w1', 'w2', 'w3')}
    del _L0_ffn_all
    return {'x': x, 'itok_BxS_13_99985': itok_BxS_13_99985, 'ctx_2048': ctx_2048, 'L0_attn_qkv': _L0_attn_in['qkv'], 'L0_attn_o_proj': _L0_attn_in['o_proj'], 'L0_attn_gamma': _L0_attn_in['gamma'], 'L0_attn_beta': _L0_attn_in['beta'], 'L0_ffn_gate_w': _L0_ffn_in['gate_w'], 'L0_ffn_w1': _L0_ffn_in['w1'], 'L0_ffn_w2': _L0_ffn_in['w2'], 'L0_ffn_w3': _L0_ffn_in['w3']}

def reference(x, itok_BxS_13_99985, ctx_2048, L0_attn_qkv, L0_attn_o_proj, L0_attn_gamma, L0_attn_beta, L0_ffn_gate_w, L0_ffn_w1, L0_ffn_w2, L0_ffn_w3):
    import jax
    import jax.numpy as jnp

    def _L0_attn_ref(x, qkv, o_proj, gamma, beta):
        import jax, jax.numpy as jnp
        import numpy as np
        HIDDEN = 256
        KEY = 256
        EPS = 1e-05
        residual = x
        mu = jnp.mean(x, axis=-1, keepdims=True)
        var = jnp.mean((x - mu) ** 2, axis=-1, keepdims=True)
        x_norm = (x - mu) / jnp.sqrt(var + EPS) * gamma + beta
        q = x_norm @ qkv[:, :KEY]
        k = x_norm @ qkv[:, KEY:2 * KEY]
        v = x_norm @ qkv[:, 2 * KEY:]
        scale = 1.0 / jnp.sqrt(jnp.float32(KEY))
        scores = jnp.einsum('bsk,btk->bst', q, k) * scale
        S_len = x.shape[1]
        causal = jnp.tril(jnp.ones((S_len, S_len), dtype=bool))
        scores = jnp.where(causal[None], scores, -jnp.inf)
        attn = jax.nn.softmax(scores, axis=-1)
        out = attn @ v
        out = out @ o_proj
        return out + residual

    def _L0_xattn_ref(hidden_states, token_ids, Wg, Wu, Wd):
        import jax, jax.numpy as jnp
        import numpy as np
        B, S, D = (4, 512, 256)
        E = 4
        F = 1024 // E
        VOCAB = 12500
        tokens_per_expert = VOCAB // E
        tid = jnp.clip(token_ids, 0, VOCAB - 1)
        expert_ids = jnp.minimum(tid // tokens_per_expert, E - 1)
        out = jnp.zeros_like(hidden_states)
        for e in range(E):
            g = jax.nn.silu(jnp.einsum('bsd,fd->bsf', hidden_states, Wg[e]))
            u = jnp.einsum('bsd,fd->bsf', hidden_states, Wu[e])
            y = jnp.einsum('bsf,df->bsd', g * u, Wd[e])
            out = jnp.where((expert_ids == e)[..., None], y, out)
        return out

    def _L0_ffn_ref(hidden_states, gate_w, w1, w2, w3):
        import jax, jax.numpy as jnp
        import numpy as np
        NUM_EXPERTS = 12
        TOP_K = 2
        FFN_DIM = 160
        HIDDEN = 256
        B, S, H = hidden_states.shape
        x = hidden_states.reshape(-1, H)
        T = x.shape[0]
        logits = x @ gate_w.T
        probs = jax.nn.softmax(logits, axis=-1)
        top_w, top_i = jax.lax.top_k(probs, TOP_K)
        top_w = top_w / jnp.sum(top_w, axis=-1, keepdims=True)
        cw = jnp.zeros((T, NUM_EXPERTS), dtype=x.dtype)
        cw = cw.at[jnp.arange(T)[:, None], top_i].add(top_w)
        out = jnp.zeros_like(x)
        for e in range(NUM_EXPERTS):
            h = jax.nn.silu(x @ w1[e].T) * (x @ w3[e].T)
            out = out + h @ w2[e].T * cw[:, e:e + 1]
        return out.reshape(B, S, H)
    x = x + _L0_attn_ref(_layernorm(x, axis=-1), L0_attn_qkv, L0_attn_o_proj, L0_attn_gamma, L0_attn_beta)
    x = x + _L0_xattn_ref(_layernorm(x, axis=-1), itok_BxS_13_99985, ctx_2048, ctx_2048, ctx_2048)
    x = x + _L0_ffn_ref(_layernorm(x, axis=-1), L0_ffn_gate_w, L0_ffn_w1, L0_ffn_w2, L0_ffn_w3)
    return x

_drawn_inputs = setup_inputs


def setup_inputs(seed=0):
    import zlib

    import numpy as np

    out = dict(_drawn_inputs(seed))
    spreads = {'L0_attn_gamma': (1.0, 0.6), 'L0_attn_beta': (0.0, 0.564)}
    factors = {'ctx_2048': 3.433,
     'L0_ffn_gate_w': 8.0,
     'L0_ffn_w1': 8.0,
     'L0_ffn_w2': 8.0,
     'L0_ffn_w3': 8.0}
    for name, (base, spread) in spreads.items():
        noise = np.random.default_rng([zlib.crc32(name.encode()), seed]).standard_normal(out[name].shape)
        drawn = base * np.exp(spread * noise) if base else spread * noise
        out[name] = jnp.asarray(drawn.astype(out[name].dtype))
    for name, factor in factors.items():
        out[name] = (out[name] * factor).astype(out[name].dtype)
    return out
```

```python
from contextlib import ExitStack

import numpy as np

import concourse.bass as bass
from concourse import mybir

F32 = mybir.dt.float32
BF16 = mybir.dt.bfloat16
I32 = mybir.dt.int32
U32 = mybir.dt.uint32
ALU = mybir.AluOpType
ACT = mybir.ActivationFunctionType
AX = mybir.AxisListType

P = 128
EPS = 1e-5
MASKED = -1e30


def decoder_layer(nc, x, ids, ctx_t, qkv_t, wo, gamma_beta, gate_t, w13_t, w2_lo_t, w2_hi_t, out):
    T, D = x.shape
    KD = D // P
    NT = T // P
    B = ids.shape[0]
    TB = NT // B
    S = T // B
    E2 = ctx_t.shape[2]
    VOCAB = 12500
    PER_EXPERT = VOCAB // E2
    E3 = gate_t.shape[2]
    TOPK = 2
    F3 = w13_t.shape[3] // 2
    F3R = F3 - P
    NT2 = T // P + E2 - 1
    NT3 = TOPK * T // P + E3 - 1
    LOOP = 4
    FIRST = 6
    assert KD == 2 and TB == 2 and D == 256 and P < F3 <= 2 * P

    with ExitStack() as stack:
        def sb(name, shape, dt=F32):
            return stack.enter_context(nc.sbuf_tensor(name, shape, dt))

        def sem(name):
            return stack.enter_context(nc.semaphore(name))

        h2_dram = nc.dram_tensor("h2_rows", [T, D], F32).ap()
        y2_dram = nc.dram_tensor("y2_rows", [T + NT2 * P, D], F32).ap()
        h3_dram = nc.dram_tensor("h3_rows", [T, D], F32).ap()
        y3_dram = nc.dram_tensor("y3_rows", [TOPK * T + NT3 * P, D], F32).ap()

        bank = [stack.enter_context(nc.psum_tensor(f"bank{i}", [P, 512], F32)) for i in range(8)]

        ident = sb("ident", [P, P])
        ident_bf = sb("ident_bf", [P, P], BF16)
        causal_bf = sb("causal_bf", [P, S], BF16)
        before_bf = sb("before_bf", [P, P], BF16)
        ones_bf = sb("ones_bf", [P, P], BF16)
        iota_slot = sb("iota_slot", [P, P])
        iota_part = sb("iota_part", [P, 1])
        iota_col = sb("iota_col", [P, TOPK * NT])
        pow_half = sb("pow_half", [P, TB])

        qkv_sb = sb("qkv_sb", [P, 3, KD, D])
        wo_sb = sb("wo_sb", [P, KD, D])
        gb_sb = sb("gb_sb", [P, 2, KD])
        qk_sb = sb("qk_sb", [P, KD, D])
        vo_sb = sb("vo_sb", [P, KD, D])
        ctx_sb = sb("ctx_sb", [P, KD, E2, D])
        gate_sb = sb("gate_sb", [P, KD, E3])
        w13_sb = sb("w13_sb", [P, KD, E3, 2 * F3])
        w2a_sb = sb("w2a_sb", [P, E3, D])
        w2b_sb = sb("w2b_sb", [F3R, E3, D])

        x_sb = sb("x_sb", [P, NT, D])
        h1_sb = sb("h1_sb", [P, NT, D])
        xn_sb = sb("xn_sb", [P, NT, D])
        xh_sb = sb("xh_sb", [P, NT, D])
        x1_sb = sb("x1_sb", [P, NT, D])
        h2_sb = xn_sb
        x2_sb = x_sb
        h3_sb = h1_sb
        y2_sb = xh_sb
        y3_sb = sb("y3_sb", [P, TOPK, NT, D])
        out_sb = x1_sb

        NORMS = 4
        stats = sb("stats", [P, NORMS, NT, 6])
        meanvar = sb("meanvar", [P, NORMS, NT, 2])
        vareps = sb("vareps", [P, NORMS, NT])
        rstd = sb("rstd", [P, NORMS, NT])

        xnT_sb = sb("xnT_sb", [P, 2, KD, S])
        pT_sb = sb("pT_sb", [P, 2, KD, S])
        vv_sb = sb("vv_sb", [P, 2, TB, D])
        prob_sb = sb("prob_sb", [P, 2, TB, S])
        probT_sb = sb("probT_sb", [P, 2, 3, P])
        negmax = sb("negmax", [P, NT])
        rowsum = sb("rowsum", [P, NT])
        rowinv = sb("rowinv", [P, NT])

        class Routing:
            def __init__(self, tag, E, C, tiles):
                self.tag, self.E, self.C, self.tiles = tag, E, C, tiles
                self.expert = sb(f"{tag}_expert", [P, C])
                self.onehot = sb(f"{tag}_onehot", [P, E, C], BF16)
                self.goes_on = sb(f"{tag}_goes_on", [P, E, C])
                self.cum = sb(f"{tag}_cum", [P, E, C])
                self.rank = sb(f"{tag}_rank", [P, E, C])
                self.ntile_i = sb(f"{tag}_ntile_i", [P, E], I32)
                self.ntile = sb(f"{tag}_ntile", [P, E])
                self.ones = sb(f"{tag}_ones", [P, E])
                self.end = sb(f"{tag}_end", [P, E])
                self.start = sb(f"{tag}_start", [P, E])
                self.slot = sb(f"{tag}_slot", [P, C])
                self.slot_i = sb(f"{tag}_slot_i", [P, 3, C], I32)
                self.slot_f = sb(f"{tag}_slot_f", [P, 2, C])
                self.at_row = sb(f"{tag}_at_row", [P, C, P], BF16)
                self.at_tile = sb(f"{tag}_at_tile", [P, C, 3, tiles], BF16)
                self.table = sb(f"{tag}_table", [P, 3, tiles])
                self.spare = sb(f"{tag}_spare", [P, tiles])
                self.unused = sb(f"{tag}_unused", [P, tiles])
                self.dest_f = sb(f"{tag}_dest_f", [P, tiles])
                self.dest = sb(f"{tag}_dest", [P, tiles], I32)
                self.src = sb(f"{tag}_src", [P, tiles], I32)
                self.past = sb(f"{tag}_past", [P, tiles, E])
                self.tile_f = sb(f"{tag}_tile_f", [P, tiles])
                self.tile_expert = sb(f"{tag}_tile_expert", [P, tiles], I32)
                self.s_onehot = sem(f"{tag}_s_onehot")
                self.s_counts = sem(f"{tag}_s_counts")
                self.s_step = sem(f"{tag}_s_step")
                self.s_rows = sem(f"{tag}_s_rows")
                self.s_table = sem(f"{tag}_s_table")
                self.s_ready = sem(f"{tag}_s_ready")

        R2 = Routing("r2", E2, NT, NT2)
        R3 = Routing("r3", E3, TOPK * NT, NT3)
        R2.psum, R2.psum_table = bank[7], bank[7][:, 64:64 + 3 * NT2]
        R3.psum, R3.psum_table = bank[4], bank[5][:, 0:3 * NT3]
        ids_sb = sb("ids_sb", [NT, P], I32)
        ids_f = sb("ids_f", [NT, P])
        top_val = sb("top_val", [P, NT, 8])
        top_idx = sb("top_idx", [P, NT, 8], U32)
        gap = sb("gap", [P, NT])
        top_w = sb("top_w", [P, TOPK, NT])
        h3T_sb = sb("h3T_sb", [P, 2, KD, P])

        rows_in = sb("rows_in", [P, 4, D])
        rowsT = sb("rowsT", [P, 2, KD, P])
        silu_sb = sb("silu_sb", [P, 2, D])
        prod_sb = sb("prod_sb", [P, 2, D])
        prodT = sb("prodT", [P, 2, 2, P])
        rows_out = sb("rows_out", [P, 4, D])

        s_ids = sem("s_ids")
        s_x = [sem(f"s_x_in{b}") for b in range(B)]
        s_wattn = sem("s_wattn")
        s_wo = sem("s_wo")
        s_gb = sem("s_gb")
        s_ctx = sem("s_ctx")
        s_gate = sem("s_gate")
        s_w13 = sem("s_w13")
        s_w2a = sem("s_w2a")
        s_w2b = sem("s_w2b")
        s_fill = sem("s_fill")
        s_ident = sem("s_ident")
        s_const = sem("s_const")
        s_qk = sem("s_qk")
        s_vo = sem("s_vo")
        s_qk_sb = sem("s_qk_sb")
        s_vo_sb = sem("s_vo_sb")
        s_stat = [sem(f"s_stat{n}") for n in range(NORMS)]
        s_mv = [sem(f"s_mv{n}") for n in range(NORMS)]
        s_var = [sem(f"s_var{n}") for n in range(NORMS)]
        s_rstd = [sem(f"s_rstd{n}") for n in range(NORMS)]
        s_norm = [sem(f"s_norm{n}") for n in range(NORMS)]
        s_xh = sem("s_xh")
        s_xnT = sem("s_xnT")
        s_xnT_sb = sem("s_xnT_sb")
        s_pT = sem("s_pT")
        s_pT_sb = sem("s_pT_sb")
        s_vv = sem("s_vv")
        s_vv_sb = sem("s_vv_sb")
        s_score = sem("s_score")
        s_max = sem("s_max")
        s_exp = sem("s_exp")
        s_probT = sem("s_probT")
        s_probT_sb = sem("s_probT_sb")
        s_inv = sem("s_inv")
        s_attn = sem("s_attn")
        s_x1 = sem("s_x1")
        s_h2_out = sem("s_h2_out")
        s_y2_in = [sem(f"s_y2_in{b}") for b in range(B)]
        s_x2 = sem("s_x2")
        s_h3_out = sem("s_h3_out")
        s_h3T = sem("s_h3T")
        s_h3T_sb = sem("s_h3T_sb")
        s_logit = sem("s_logit")
        s_max8 = sem("s_max8")
        s_idx8 = sem("s_idx8")
        s_gap = sem("s_gap")
        s_topw = sem("s_topw")
        s_idsf = sem("s_idsf")
        s_idsT = sem("s_idsT")
        s_y3_in = [sem(f"s_y3_in{b}") for b in range(B)]
        s_mix = sem("s_mix")
        s_sum = sem("s_sum")
        s_out = sem("s_out")

        class ExpertBlock:
            def __init__(self, tag, routing, first_w, first_n, width, second_w, src, dst):
                self.routing, self.tiles = routing, routing.tiles
                self.first_w, self.first_n, self.width = first_w, first_n, width
                self.second_w, self.src, self.dst = second_w, src, dst
                self.s_in = [sem(f"{tag}_in{m}") for m in range(4)]
                self.s_rowsT = sem(f"{tag}_rowsT")
                self.s_rowsT_sb = sem(f"{tag}_rowsT_sb")
                self.s_first = sem(f"{tag}_first")
                self.s_silu = sem(f"{tag}_silu")
                self.s_prod = sem(f"{tag}_prod")
                self.s_prodT = sem(f"{tag}_prodT")
                self.s_prodT_sb = sem(f"{tag}_prodT_sb")
                self.s_rest_sb = sem(f"{tag}_rest_sb")
                self.s_second = sem(f"{tag}_second")
                self.s_y = sem(f"{tag}_y")
                self.s_done = [sem(f"{tag}_done{m}") for m in range(4)]

            def scattered(self, eng):
                for m in range(4):
                    eng.wait_ge(self.s_done[m], 16 * len(range(m, self.tiles, 4)))

        X2 = ExpertBlock("x2", R2, ctx_sb, D, D, [ctx_sb[:, k] for k in range(KD)], h2_dram, y2_dram)
        X3 = ExpertBlock("x3", R3, w13_sb, 2 * F3, F3, [w2a_sb, w2b_sb], h3_dram, y3_dram)

        def pipeline(eng, tiles, step):
            def at(i):
                step(i, i % LOOP, i // LOOP, i)
            turns = (tiles - 1 - FIRST) // LOOP
            if turns < 2:
                turns = 0
            for i in range(FIRST):
                at(i)
            if turns:
                with eng.Fori(0, turns) as n:
                    for u in range(FIRST, FIRST + LOOP):
                        step(n * LOOP + u, u % LOOP, n + u // LOOP, None)
            for i in range(FIRST + LOOP * turns, tiles + 2):
                at(i)

        block = stack.enter_context(nc.Block())

        @block.sync
        def _(sp):
            sp.dma_start(ids_sb[:, :], ids.rearrange("b (c p) -> (b c) p", p=P)).then_inc(s_ids, 16)
            rows = x.rearrange("(c p) d -> p c d", p=P)
            sp.dma_start(x_sb[:, 0:TB, :], rows[:, 0:TB, :]).then_inc(s_x[0], 16)
            sp.dma_start(qkv_sb[:, :, :, :], qkv_t).then_inc(s_wattn, 16)
            sp.dma_start(wo_sb[:, :, :], wo).then_inc(s_wo, 16)
            sp.dma_start(gb_sb[:, :, :], gamma_beta).then_inc(s_gb, 16)
            for b in range(1, B):
                sp.dma_start(x_sb[:, b * TB:(b + 1) * TB, :], rows[:, b * TB:(b + 1) * TB, :]).then_inc(s_x[b], 16)
            sp.dma_start(ctx_sb[:, :, :, :], ctx_t).then_inc(s_ctx, 16)
            sp.dma_start(gate_sb[:, :, :], gate_t).then_inc(s_gate, 16)
            sp.dma_start(w13_sb[:, :, :, :], w13_t).then_inc(s_w13, 16)
            sp.dma_start(w2a_sb[:, :, :], w2_lo_t).then_inc(s_w2a, 16)
            sp.dma_start(w2b_sb[:, :, :], w2_hi_t).then_inc(s_w2b, 16)
            h2_rows = h2_dram.rearrange("(c p) d -> p c d", p=P)
            h3_rows = h3_dram.rearrange("(c p) d -> p c d", p=P)
            for b in range(B):
                sp.wait_ge(s_norm[2], TB * (b + 1))
                sp.dma_start(h2_rows[:, b * TB:(b + 1) * TB, :], h2_sb[:, b * TB:(b + 1) * TB, :]).then_inc(s_h2_out, 16)
            X2.scattered(sp)
            y2_rows = y2_dram[0:T, :].rearrange("(c p) d -> p c d", p=P)
            for b in range(B):
                sp.dma_start(y2_sb[:, b * TB:(b + 1) * TB, :], y2_rows[:, b * TB:(b + 1) * TB, :]).then_inc(s_y2_in[b], 16)
            for b in range(B):
                sp.wait_ge(s_norm[3], TB * (b + 1))
                sp.dma_start(h3_rows[:, b * TB:(b + 1) * TB, :], h3_sb[:, b * TB:(b + 1) * TB, :]).then_inc(s_h3_out, 16)
            X3.scattered(sp)
            y3_rows = y3_dram[0:TOPK * T, :].rearrange("(k c p) d -> p k c d", k=TOPK, p=P)
            for b in range(B):
                for k in range(TOPK):
                    sp.dma_start(y3_sb[:, k, b * TB:(b + 1) * TB, :], y3_rows[:, k, b * TB:(b + 1) * TB, :]).then_inc(s_y3_in[b], 16)
            out_rows = out.rearrange("(c p) d -> p c d", p=P)
            for b in range(B):
                sp.wait_ge(s_sum, TB * (b + 1))
                sp.dma_start(out_rows[:, b * TB:(b + 1) * TB, :], out_sb[:, b * TB:(b + 1) * TB, :]).then_inc(s_out, 16)
            sp.wait_ge(s_out, 16 * B)

        @block.gpsimd
        def _(pool):
            pool.memset(ident[:, :], 0.0).then_inc(s_fill, 1)
            pool.memset(pow_half[:, :], -0.5).then_inc(s_fill, 1)
            pool.wait_ge(s_fill, 1)
            pool.affine_select(out=ident[:, :], in_=ident[:, :], compare_op=ALU.not_equal, fill=1.0, base=0,
                               pattern=[[-1, P]], channel_multiplier=1).then_inc(s_ident, 1)
            pool.memset(causal_bf[:, :], 0.0).then_inc(s_fill, 1)
            pool.memset(before_bf[:, :], 1.0).then_inc(s_fill, 1)
            pool.memset(ones_bf[:, :], 1.0).then_inc(s_fill, 1)
            pool.wait_ge(s_ident, 1)
            pool.tensor_copy(ident_bf[:, :], ident[:, :]).then_inc(s_const, 1)
            pool.wait_ge(s_fill, 5)
            pool.affine_select(out=causal_bf[:, :], in_=causal_bf[:, :], compare_op=ALU.is_ge, fill=MASKED, base=S - P,
                               pattern=[[-1, S]], channel_multiplier=1).then_inc(s_const, 1)
            pool.affine_select(out=before_bf[:, :], in_=before_bf[:, :], compare_op=ALU.is_gt, fill=0.0, base=0,
                               pattern=[[1, P]], channel_multiplier=-1).then_inc(s_const, 1)
            pool.iota(iota_slot[:, :], pattern=[[1, P]], base=0, channel_multiplier=0,
                      allow_small_or_imprecise_dtypes=True).then_inc(s_const, 1)
            pool.iota(iota_part[:, :], pattern=[[0, 1]], base=0, channel_multiplier=1,
                      allow_small_or_imprecise_dtypes=True).then_inc(s_const, 1)
            pool.iota(iota_col[:, :], pattern=[[1, TOPK * NT]], base=0, channel_multiplier=0,
                      allow_small_or_imprecise_dtypes=True).then_inc(s_const, 1)

            for R in (R2, R3):
                pool.iota(R.spare[:, :], pattern=[[P, R.tiles]], base=R.C * P, channel_multiplier=1,
                          allow_small_or_imprecise_dtypes=True).then_inc(s_const, 1)

            def inverse_root(n, b):
                pool.wait_ge(s_var[n], b + 1)
                pool.tensor_tensor(rstd[:, n, b * TB:(b + 1) * TB], vareps[:, n, b * TB:(b + 1) * TB], pow_half[:, :],
                                   ALU.pow).then_inc(s_rstd[n], 1)

            def residual(b):
                pool.wait_ge(s_norm[0], TB * (b + 1))
                pool.tensor_tensor(xh_sb[:, b * TB:(b + 1) * TB, :], x_sb[:, b * TB:(b + 1) * TB, :],
                                   h1_sb[:, b * TB:(b + 1) * TB, :], ALU.add).then_inc(s_xh, 1)

            def route_by_slot(blk):
                def gather(j):
                    if j >= 4:
                        pool.wait_ge(blk.s_rowsT, j - 3)
                    pool.indirect_dma_start(
                        out=rows_in[:, j % 4, :], out_offset=None, in_=blk.src,
                        in_offset=bass.IndirectOffsetOnAxis(ap=blk.routing.src[:, j:j + 1].bitcast(U32), axis=0),
                    ).then_inc(blk.s_in[j % 4], 16)

                def scatter(j):
                    pool.wait_ge(blk.s_y, j + 1)
                    pool.indirect_dma_start(
                        out=blk.dst, in_=rows_out[:, j % 4, :], in_offset=None,
                        out_offset=bass.IndirectOffsetOnAxis(ap=blk.routing.dest[:, j:j + 1].bitcast(U32), axis=0),
                    ).then_inc(blk.s_done[j % 4], 16)

                for j in range(4):
                    gather(j)
                for j in range(blk.tiles):
                    if j + 4 < blk.tiles:
                        gather(j + 4)
                    scatter(j)

            inverse_root(0, 0)
            inverse_root(0, 1)
            inverse_root(1, 0)
            inverse_root(1, 1)
            residual(0)
            residual(1)
            for b in range(B):
                if b + 2 < B:
                    inverse_root(0, b + 2)
                inverse_root(2, b)
                if b + 2 < B:
                    inverse_root(1, b + 2)
                    residual(b + 2)
            pool.wait_ge(s_h2_out, 16 * B)
            pool.wait_ge(R2.s_ready, 1)
            route_by_slot(X2)
            for b in range(B):
                inverse_root(3, b)
            pool.wait_ge(s_h3_out, 16 * B)
            pool.wait_ge(R3.s_ready, 1)
            route_by_slot(X3)

        @block.vector
        def _(dve):
            dve.memset(R2.ones[:, :], 1.0).then_inc(R2.s_step, 1)
            dve.memset(R3.ones[:, :], 1.0).then_inc(R3.s_step, 1)
            for R in (R2, R3):
                dve.memset(R.goes_on[:, :, :], 1.0).then_inc(R.s_step, 1)
            dve.wait_ge(R2.s_step, 2)
            dve.memset(R2.goes_on[:, :, 0:1], 0.0).then_inc(R2.s_step, 1)
            dve.wait_ge(R3.s_step, 2)
            dve.memset(R3.goes_on[:, :, 0:1], 0.0).then_inc(R3.s_step, 1)

            def moments(n, src, b):
                ts = range(b * TB, (b + 1) * TB)
                for t in ts:
                    dve.bn_stats(stats[:, n, t, :], src[:, t, :]).then_inc(s_stat[n], 1)
                for t in ts:
                    dve.wait_ge(s_stat[n], t + 1)
                    dve.bn_aggr(meanvar[:, n, t, :], stats[:, n, t, :]).then_inc(s_mv[n], 1)
                dve.wait_ge(s_mv[n], TB * (b + 1))
                dve.tensor_scalar(vareps[:, n, b * TB:(b + 1) * TB], meanvar[:, n, b * TB:(b + 1) * TB, 1], EPS, None,
                                  ALU.add).then_inc(s_var[n], 1)

            def normalise(n, dst, src, b):
                dve.wait_ge(s_rstd[n], b + 1)
                for t in range(b * TB, (b + 1) * TB):
                    dve.tensor_scalar(dst[:, t, :], src[:, t, :], meanvar[:, n, t, 0:1], rstd[:, n, t:t + 1],
                                      ALU.subtract, ALU.mult).then_inc(s_norm[n], 1)

            def norm_a(b):
                dve.wait_ge(s_x[b], 16)
                moments(0, x_sb, b)

            def norm_b(b):
                normalise(0, h1_sb, x_sb, b)
                dve.wait_ge(s_norm[0], TB * (b + 1))
                moments(1, h1_sb, b)

            def norm_c(b):
                normalise(1, xn_sb, h1_sb, b)

            def row_max(b):
                for i in range(TB):
                    t = b * TB + i
                    dve.wait_ge(s_score, t + 1)
                    dve.tensor_reduce(negmax[:, t:t + 1], bank[3 + i][:, 0:(i + 1) * P], AX.X, ALU.max,
                                      negate=True).then_inc(s_max, 1)

            def prob_transposed(b):
                dve.wait_ge(s_probT, b + 1)
                if b >= 2:
                    dve.wait_ge(s_attn, b - 1)
                dve.tensor_copy(probT_sb[:, b % 2, :, :], bank[5][:, 0:3 * P]).then_inc(s_probT_sb, 1)
                dve.wait_ge(s_exp, TB * (b + 1))
                dve.reciprocal(rowinv[:, b * TB:(b + 1) * TB], rowsum[:, b * TB:(b + 1) * TB]).then_inc(s_inv, 1)

            def attention_out(b):
                dve.wait_ge(s_attn, b + 1)
                dve.wait_ge(s_inv, b + 1)
                dve.wait_ge(s_xh, b + 1)
                for i in range(TB):
                    t = b * TB + i
                    dve.scalar_tensor_tensor(out=x1_sb[:, t, :], in0=bank[6][:, i * D:(i + 1) * D],
                                             scalar=rowinv[:, t:t + 1], in1=xh_sb[:, t, :], op0=ALU.mult,
                                             op1=ALU.add).then_inc(s_x1, 1)
                dve.wait_ge(s_x1, TB * (b + 1))
                moments(2, x1_sb, b)

            def token_experts():
                dve.wait_ge(s_idsT, 1)
                for e in range(1, E2):
                    if e == 1:
                        ins = dve.tensor_scalar(R2.expert[:, :], bank[7][:, 0:NT], float(PER_EXPERT), None, ALU.is_ge)
                    else:
                        dve.wait_ge(R2.s_step, 3 + e - 1)
                        ins = dve.scalar_tensor_tensor(out=R2.expert[:, :], in0=bank[7][:, 0:NT],
                                                       scalar=float(e * PER_EXPERT), in1=R2.expert[:, :],
                                                       op0=ALU.is_ge, op1=ALU.add)
                    ins.then_inc(R2.s_step, 1)
                dve.wait_ge(R2.s_step, 3 + E2 - 1)

            def slots(R, done):
                n = [done]

                def step(ins):
                    n[0] += 1
                    ins.then_inc(R.s_step, 1)

                def join():
                    dve.wait_ge(R.s_step, n[0])
                E, C, NTL = R.E, R.C, R.tiles
                dve.tensor_tensor(R.onehot[:, :, :], iota_slot[:, 0:E].rearrange("p (e o) -> p e o", o=1).to_broadcast([P, E, C]),
                                  R.expert[:, :].rearrange("p (o c) -> p o c", o=1).to_broadcast([P, E, C]),
                                  ALU.is_equal).then_inc(R.s_onehot, 1)
                dve.wait_ge(R.s_counts, 1)
                in_tile = R.psum[:, 0:E * C]
                totals = R.psum[:, 256:256 + E * C]
                flat = lambda a: a[:, :, :].rearrange("p e c -> p (e c)")
                step(dve.tensor_tensor_scan(flat(R.cum), flat(R.goes_on), totals, 0.0, ALU.mult, ALU.add))
                join()
                step(dve.tensor_tensor(flat(R.rank), flat(R.cum), totals, ALU.subtract))
                step(dve.tensor_scalar(R.ntile_i[:, :], R.cum[:, :, C - 1], float(P - 1), None, ALU.add))
                join()
                step(dve.tensor_tensor(flat(R.rank), flat(R.rank), in_tile, ALU.add))
                step(dve.tensor_scalar(R.ntile_i[:, :], R.ntile_i[:, :], 7, None, ALU.arith_shift_right))
                join()
                step(dve.tensor_copy(R.ntile[:, :], R.ntile_i[:, :]))
                join()
                step(dve.tensor_tensor_scan(R.end[:, :], R.ones[:, :], R.ntile[:, :], 0.0, ALU.mult, ALU.add))
                join()
                step(dve.tensor_tensor(R.start[:, :], R.end[:, :], R.ntile[:, :], ALU.subtract))
                step(dve.tensor_tensor(R.past[:, :, :],
                                       iota_slot[:, 0:NTL].rearrange("p (j o) -> p j o", o=1).to_broadcast([P, NTL, E]),
                                       R.end[:, :].rearrange("p (o e) -> p o e", o=1).to_broadcast([P, NTL, E]), ALU.is_ge))
                join()
                step(dve.tensor_reduce(R.tile_f[:, :], R.past[:, :, :], AX.X, ALU.add))
                step(dve.scalar_tensor_tensor(out=R.rank[:, :, :],
                                              in0=R.start[:, :].rearrange("p (e o) -> p e o", o=1).to_broadcast([P, E, C]),
                                              scalar=float(P), in1=R.rank[:, :, :], op0=ALU.mult, op1=ALU.add))
                join()
                step(dve.tensor_scalar(R.tile_expert[:, :], R.tile_f[:, :], float(E - 1), None, ALU.min))
                step(dve.tensor_tensor(R.rank[:, :, :], R.rank[:, :, :], R.onehot[:, :, :], ALU.mult))
                join()
                step(dve.tensor_reduce(R.slot[:, :], R.rank[:, :, :].rearrange("p e c -> p c e"), AX.X, ALU.add))
                join()
                step(dve.tensor_copy(R.slot_i[:, 0, :], R.slot[:, :]))
                join()
                step(dve.tensor_scalar(R.slot_i[:, 1, :], R.slot_i[:, 0, :], P - 1, None, ALU.bitwise_and))
                step(dve.tensor_scalar(R.slot_i[:, 2, :], R.slot_i[:, 0, :], 7, None, ALU.arith_shift_right))
                join()
                step(dve.tensor_copy(R.slot_f[:, :, :], R.slot_i[:, 1:3, :]))
                join()
                step(dve.tensor_tensor(R.at_tile[:, :, 2, :],
                                       iota_slot[:, 0:NTL].rearrange("p (o j) -> p o j", o=1).to_broadcast([P, C, NTL]),
                                       R.slot_f[:, 1, :].rearrange("p (c o) -> p c o", o=1).to_broadcast([P, C, NTL]),
                                       ALU.is_equal))
                join()
                step(dve.tensor_scalar(R.at_tile[:, :, 0, :], R.at_tile[:, :, 2, :], iota_part[:, 0:1], None, ALU.mult))
                step(dve.tensor_tensor(R.at_tile[:, :, 1, :], R.at_tile[:, :, 2, :],
                                       iota_col[:, 0:C].rearrange("p (c o) -> p c o", o=1).to_broadcast([P, C, NTL]),
                                       ALU.mult))
                for half in range(2):
                    cs = slice(half * C // 2, (half + 1) * C // 2)
                    dve.tensor_tensor(R.at_row[:, cs, :],
                                      iota_slot[:, :].rearrange("p (o q) -> p o q", o=1).to_broadcast([P, C // 2, P]),
                                      R.slot_f[:, 0, cs].rearrange("p (c o) -> p c o", o=1).to_broadcast([P, C // 2, P]),
                                      ALU.is_equal).then_inc(R.s_rows, 1)
                dve.wait_ge(R.s_table, 1)
                step(dve.tensor_copy(R.table[:, :, :], R.psum_table))
                join()
                step(dve.scalar_tensor_tensor(out=R.dest_f[:, :], in0=R.table[:, 1, :], scalar=float(P),
                                              in1=R.table[:, 0, :], op0=ALU.mult, op1=ALU.add))
                step(dve.scalar_tensor_tensor(out=R.unused[:, :], in0=R.table[:, 2, :], scalar=0.0, in1=R.spare[:, :],
                                              op0=ALU.is_equal, op1=ALU.mult))
                join()
                step(dve.tensor_tensor(R.dest[:, :], R.dest_f[:, :], R.unused[:, :], ALU.add))
                join()
                dve.tensor_scalar(R.src[:, :], R.dest[:, :], T - 1, None, ALU.bitwise_and).then_inc(R.s_ready, 1)

            def expert_vector(blk):
                factor0 = blk.first_n - blk.width

                def step(i, m, q, known):
                    def rows_transposed(j, mj):
                        dve.wait_ge(blk.s_rowsT, j + 1)
                        if known is None or known >= 1:
                            dve.wait_ge(blk.s_first, j - 1)
                        dve.tensor_copy(rowsT[:, mj % 2, :, :], bank[mj % 2][:, 0:D]).then_inc(blk.s_rowsT_sb, 1)

                    if known == 0:
                        dve.wait_ge(blk.s_rowsT, 1)
                        dve.tensor_copy(rowsT[:, 0, :, :], bank[0][:, 0:D]).then_inc(blk.s_rowsT_sb, 1)
                    if known is None or known + 1 < blk.tiles:
                        rows_transposed(i + 1, m + 1)
                    if blk is X3 and (known is None or 2 <= known):
                        dve.wait_ge(blk.s_prodT, i - 1)
                        if known is None or known >= 4:
                            dve.wait_ge(blk.s_second, i - 3)
                        dve.tensor_copy(prodT[0:F3R, m % 2, 1, :], bank[m % 2][0:F3R, D:D + P]).then_inc(blk.s_rest_sb, 1)
                    if known is None or known < blk.tiles:
                        dve.wait_ge(blk.s_silu, i + 1)
                        if known is None or known >= 2:
                            dve.wait_ge(blk.s_prodT, i - 1)
                        dve.tensor_tensor(prod_sb[:, m % 2, 0:blk.width], silu_sb[:, m % 2, 0:blk.width],
                                          bank[2 + m % 2][:, factor0:factor0 + blk.width], ALU.mult).then_inc(blk.s_prod, 1)
                pipeline(dve, blk.tiles, step)

            norm_a(0)
            norm_a(1)
            norm_b(0)
            norm_b(1)
            norm_c(0)
            dve.wait_ge(s_ids, 16)
            dve.tensor_copy(ids_f[:, :], ids_sb[:, :]).then_inc(s_idsf, 1)
            for b in range(B):
                if b == 0:
                    token_experts()
                row_max(b)
                if b + 1 < B:
                    norm_c(b + 1)
                prob_transposed(b)
                if b + 2 < B:
                    norm_a(b + 2)
                if b == 0:
                    dve.wait_ge(s_const, 8)
                    slots(R2, 3 + E2 - 1)
                attention_out(b)
                if b + 2 < B:
                    norm_b(b + 2)
                normalise(2, h2_sb, x1_sb, b)
            expert_vector(X2)

            def best_two(t):
                dve.wait_ge(s_logit, t + 1)
                lg = bank[2 + t % 2][:, 0:E3]
                dve.max(top_val[:, t, :], lg).then_inc(s_max8, 1)
                dve.wait_ge(s_max8, t + 1)
                dve.max_index(top_idx[:, t, :], top_val[:, t, :], lg).then_inc(s_idx8, 1)

            def second_residual(b):
                dve.wait_ge(s_y2_in[b], 16)
                dve.tensor_tensor(x2_sb[:, b * TB:(b + 1) * TB, :], x1_sb[:, b * TB:(b + 1) * TB, :],
                                  y2_sb[:, b * TB:(b + 1) * TB, :], ALU.add).then_inc(s_x2, 1)
                dve.wait_ge(s_x2, b + 1)
                moments(3, x2_sb, b)

            second_residual(0)
            for b in range(B):
                if b + 1 < B:
                    second_residual(b + 1)
                normalise(3, h3_sb, x2_sb, b)
                if b >= 1:
                    best_two(TB * b - 2)
                    best_two(TB * b - 1)
            best_two(NT - 2)
            best_two(NT - 1)
            dve.wait_ge(s_idx8, NT)
            dve.tensor_copy(R3.expert[:, :].rearrange("p (k t) -> p t k", k=TOPK), top_idx[:, :, 0:TOPK]).then_inc(R3.s_step, 1)
            dve.tensor_tensor(gap[:, :], top_val[:, :, 0], top_val[:, :, 1], ALU.subtract).then_inc(s_gap, 1)
            dve.wait_ge(R3.s_step, 4)
            slots(R3, 4)
            expert_vector(X3)

            for b in range(B):
                ts = range(b * TB, (b + 1) * TB)
                dve.wait_ge(s_y3_in[b], 16 * TOPK)
                if b == 0:
                    dve.wait_ge(s_topw, TOPK)
                for t in ts:
                    dve.scalar_tensor_tensor(out=out_sb[:, t, :], in0=y3_sb[:, 0, t, :], scalar=top_w[:, 0, t:t + 1],
                                             in1=x2_sb[:, t, :], op0=ALU.mult, op1=ALU.add).then_inc(s_mix, 1)
                for t in ts:
                    dve.wait_ge(s_mix, t + 1)
                    dve.scalar_tensor_tensor(out=out_sb[:, t, :], in0=y3_sb[:, 1, t, :], scalar=top_w[:, 1, t:t + 1],
                                             in1=out_sb[:, t, :], op0=ALU.mult, op1=ALU.add).then_inc(s_sum, 1)

        @block.scalar
        def _(act):
            act.wait_ge(s_qk, 1)
            act.activation(qk_sb[:, :, :], bank[3][:, :], ACT.Copy).then_inc(s_qk_sb, 1)
            act.wait_ge(s_vo, 1)
            act.activation(vo_sb[:, :, :], bank[4][:, :], ACT.Copy).then_inc(s_vo_sb, 1)

            def xn_transposed(b):
                act.wait_ge(s_xnT, b + 1)
                if b == 0:
                    act.wait_ge(s_gb, 16)
                if b >= 2:
                    act.wait_ge(s_score, TB * (b - 1))
                for k in range(KD):
                    act.activation(xnT_sb[:, b % 2, k, :], bank[0][:, k * S:(k + 1) * S], ACT.Identity,
                                   bias=gb_sb[:, 1, k:k + 1], scale=gb_sb[:, 0, k:k + 1]).then_inc(s_xnT_sb, 1)

            def projections(b):
                act.wait_ge(s_pT, b + 1)
                if b >= 2:
                    act.wait_ge(s_score, TB * (b - 1))
                act.activation(pT_sb[:, b % 2, :, :], bank[1][:, :], ACT.Copy, scale=float(D) ** -0.5).then_inc(s_pT_sb, 1)
                act.wait_ge(s_vv, b + 1)
                if b >= 2:
                    act.wait_ge(s_attn, b - 1)
                act.activation(vv_sb[:, b % 2, :, :], bank[2][:, :], ACT.Copy).then_inc(s_vv_sb, 1)

            def exponentials(b):
                for i in range(TB):
                    t = b * TB + i
                    act.wait_ge(s_max, t + 1)
                    if b >= 2 and i == 0:
                        act.wait_ge(s_probT, b - 1)
                    act.activation(prob_sb[:, b % 2, i, 0:(i + 1) * P], bank[3 + i][:, 0:(i + 1) * P],
                                   ACT.Exp, bias=negmax[:, t:t + 1], accum_out=rowsum[:, t:t + 1]).then_inc(s_exp, 1)

            xn_transposed(0)
            projections(0)
            for b in range(B):
                exponentials(b)
                if b + 1 < B:
                    xn_transposed(b + 1)
                    projections(b + 1)

            def expert_scalar(blk):
                def step(i, m, q, known):
                    if known is None or known >= 2:
                        act.wait_ge(blk.s_prodT, i - 1)
                        if known is None or known >= 4:
                            act.wait_ge(blk.s_second, i - 3)
                        n = D if blk is X2 else P
                        act.activation(prodT[:, m % 2, 0:n // P, :], bank[4 + m % 2][:, 0:n], ACT.Copy).then_inc(blk.s_prodT_sb, 1)
                    if known is None or known < blk.tiles:
                        act.wait_ge(blk.s_first, i + 1)
                        if known is None or known >= 2:
                            act.wait_ge(blk.s_prod, i - 1)
                        act.activation(silu_sb[:, m % 2, 0:blk.width], bank[2 + m % 2][:, 0:blk.width], ACT.Silu).then_inc(blk.s_silu, 1)
                    if known is None or known >= 2:
                        act.wait_ge(blk.s_second, i - 1)
                        if known is None or known >= 6:
                            act.wait_ge(blk.s_done[(m + 2) % 4], (q - (1 if m < 2 else 0)) * 16)
                        act.activation(rows_out[:, (m + 2) % 4, :], bank[6 + m % 2][:, 0:D], ACT.Copy).then_inc(blk.s_y, 1)
                pipeline(act, blk.tiles, step)

            expert_scalar(X2)
            for t in range(NT):
                act.wait_ge(s_h3T, t + 1)
                if t >= 2:
                    act.wait_ge(s_logit, t - 1)
                act.activation(h3T_sb[:, t % 2, :, :], bank[t % 2][:, 0:D], ACT.Copy).then_inc(s_h3T_sb, 1)
            act.wait_ge(s_gap, 1)
            for k in range(TOPK):
                act.activation(top_w[:, k, :], gap[:, :], ACT.Sigmoid, scale=1.0 - 2.0 * k).then_inc(s_topw, 1)
            expert_scalar(X3)

        @block.tensor
        def _(pe):
            def product(dst, lhs, rhs, signal=None):
                for k, (a, c) in enumerate(zip(lhs, rhs)):
                    ins = pe.matmul(dst, a, c, start=(k == 0), stop=(k == len(lhs) - 1))
                if signal is not None:
                    ins.then_inc(signal, 1)

            def cols(a, k):
                return a[:, k * P:(k + 1) * P]

            pe.wait_ge(s_wattn, 16)
            for i in range(KD):
                product(bank[3][:, i * D:(i + 1) * D], [cols(qkv_sb[:, 0, k, :], i) for k in range(KD)],
                        [qkv_sb[:, 1, k, :] for k in range(KD)], s_qk if i == KD - 1 else None)
            pe.wait_ge(s_wo, 16)
            for i in range(KD):
                product(bank[4][:, i * D:(i + 1) * D], [cols(qkv_sb[:, 2, k, :], i) for k in range(KD)],
                        [wo_sb[:, k, :] for k in range(KD)], s_vo if i == KD - 1 else None)

            def transpose_xn(b):
                pe.wait_ge(s_norm[1], TB * (b + 1))
                if b == 0:
                    pe.wait_ge(s_ident, 1)
                else:
                    pe.wait_ge(s_xnT_sb, KD * b)
                for k in range(KD):
                    for i in range(TB):
                        ins = pe.transpose(bank[0][:, k * S + i * P:k * S + (i + 1) * P], cols(xn_sb[:, b * TB + i, :], k), ident[:, :])
                ins.then_inc(s_xnT, 1)

            def project(b):
                xT = xnT_sb[:, b % 2]
                pe.wait_ge(s_xnT_sb, KD * (b + 1))
                if b == 0:
                    pe.wait_ge(s_qk_sb, 1)
                else:
                    pe.wait_ge(s_pT_sb, b)
                for j in range(KD):
                    product(bank[1][:, j * S:(j + 1) * S], [cols(qk_sb[:, k, :], j) for k in range(KD)],
                            [xT[:, k, :] for k in range(KD)], s_pT if j == KD - 1 else None)
                if b == 0:
                    pe.wait_ge(s_vo_sb, 1)
                else:
                    pe.wait_ge(s_vv_sb, b)
                for i in range(TB):
                    product(bank[2][:, i * D:(i + 1) * D], [cols(xT[:, k, :], i) for k in range(KD)],
                            [vo_sb[:, k, :] for k in range(KD)], s_vv if i == TB - 1 else None)

            def scores(b):
                xT, pT = xnT_sb[:, b % 2], pT_sb[:, b % 2]
                pe.wait_ge(s_pT_sb, b + 1)
                if b == 0:
                    pe.wait_ge(s_const, 2)
                if b >= 1:
                    pe.wait_ge(s_exp, TB * b)
                for i in range(TB):
                    n = (i + 1) * P
                    dst = bank[3 + i]
                    pe.matmul(dst[:, 0:n], ident_bf[:, :], causal_bf[:, S - n:S], start=True, stop=False)
                    for k in range(KD):
                        ins = pe.matmul(dst[:, 0:n], cols(pT[:, k, :], i), xT[:, k, 0:n], start=False,
                                        stop=(k == KD - 1))
                    ins.then_inc(s_score, 1)

            def transpose_probs(b):
                pe.wait_ge(s_exp, TB * (b + 1))
                if b >= 1:
                    pe.wait_ge(s_probT_sb, b)
                for n, (i, j) in enumerate(((0, 0), (1, 0), (1, 1))):
                    ins = pe.transpose(bank[5][:, n * P:(n + 1) * P], cols(prob_sb[:, b % 2, i, :], j), ident[:, :])
                ins.then_inc(s_probT, 1)

            def attend(b):
                pe.wait_ge(s_probT_sb, b + 1)
                pe.wait_ge(s_vv_sb, b + 1)
                if b >= 1:
                    pe.wait_ge(s_x1, TB * b)
                vv, pT = vv_sb[:, b % 2], probT_sb[:, b % 2]
                product(bank[6][:, 0:D], [pT[:, 0, :]], [vv[:, 0, :]])
                product(bank[6][:, D:2 * D], [pT[:, 1, :], pT[:, 2, :]], [vv[:, 0, :], vv[:, 1, :]], s_attn)

            def slot_counts(R):
                pe.wait_ge(R.s_onehot, 1)
                flat = R.onehot[:, :, :].rearrange("p e c -> p (e c)")
                pe.matmul(R.psum[:, 0:R.E * R.C], before_bf[:, :], flat, start=True, stop=True)
                pe.matmul(R.psum[:, 256:256 + R.E * R.C], ones_bf[:, :], flat, start=True, stop=True).then_inc(R.s_counts, 1)

            def slot_table(R):
                for c in range(R.C):
                    if c % (R.C // 2) == 0:
                        pe.wait_ge(R.s_rows, c // (R.C // 2) + 1)
                    ins = pe.matmul(R.psum_table, R.at_row[:, c, :], R.at_tile[:, c, :, :].rearrange("p a j -> p (a j)"),
                                    start=(c == 0), stop=(c == R.C - 1))
                ins.then_inc(R.s_table, 1)

            def expert_tensor(blk):
                experts = blk.routing.tile_expert

                def load_expert(j):
                    return pe.value_load(experts[0:1, bass.ds(j, 1)], min_val=0, max_val=blk.routing.E - 1)

                def rows_transpose(j, m, q, known):
                    pe.wait_ge(blk.s_in[m % 4], q * 16)
                    if known is None or known >= 2:
                        pe.wait_ge(blk.s_rowsT_sb, j - 1)
                    if blk is X3 and (known is None or known >= 4):
                        pe.wait_ge(blk.s_rest_sb, j - 3)
                    for k in range(KD):
                        ins = pe.transpose(bank[m % 2][:, k * P:(k + 1) * P], cols(rows_in[:, m % 4, :], k), ident[:, :])
                    ins.then_inc(blk.s_rowsT, 1)

                def step(i, m, q, known):
                    if known == 0:
                        rows_transpose(0, 0, 1, 0)
                    if known is None or known >= 2:
                        pe.wait_ge(blk.s_prod, i - 1)
                        if known is None or known >= 4:
                            pe.wait_ge(blk.s_prodT_sb, i - 3)
                            if blk is X3:
                                pe.wait_ge(blk.s_rest_sb, i - 3)
                        src, dst = prod_sb[:, m % 2], bank[4 + m % 2]
                        pe.transpose(dst[:, 0:P], src[:, 0:P], ident[:, :])
                        if blk is X2:
                            rest = dst[:, P:2 * P]
                        else:
                            rest = bank[m % 2][0:blk.width - P, D:D + P]
                            if known is None or known < blk.tiles:
                                pe.wait_ge(blk.s_rowsT_sb, i + 1)
                        pe.transpose(rest, src[:, P:blk.width], ident[:, :]).then_inc(blk.s_prodT, 1)
                    if known is None or known + 1 < blk.tiles:
                        rows_transpose(i + 1, (m + 1) % 4, q + (2 if m == 3 else 1), None if known is None else known + 1)
                    if known is None or known < blk.tiles:
                        e = load_expert(i)
                        pe.wait_ge(blk.s_rowsT_sb, i + 1)
                        if known is None or known >= 2:
                            pe.wait_ge(blk.s_prod, i - 1)
                        product(bank[2 + m % 2][:, 0:blk.first_n], [rowsT[:, m % 2, k, :] for k in range(KD)],
                                [blk.first_w[:, k, bass.ds(e, 1), :] for k in range(KD)], blk.s_first)
                    if known is None or known >= 2:
                        e = load_expert(i - 2)
                        pe.wait_ge(blk.s_prodT_sb, i - 1)
                        if blk is X3:
                            pe.wait_ge(blk.s_rest_sb, i - 1)
                        if known is None or known >= 4:
                            pe.wait_ge(blk.s_y, i - 3)
                        rest = blk.width - P
                        product(bank[6 + m % 2][:, 0:D], [prodT[:, m % 2, 0, :], prodT[0:rest, m % 2, 1, :]],
                                [blk.second_w[0][:, bass.ds(e, 1), :], blk.second_w[1][:, bass.ds(e, 1), :]], blk.s_second)
                pipeline(pe, blk.tiles, step)

            transpose_xn(0)
            pe.wait_ge(s_idsf, 1)
            pe.transpose(bank[7][:, 0:NT], ids_f[:, :], ident[0:NT, 0:NT]).then_inc(s_idsT, 1)
            project(0)
            for b in range(B):
                scores(b)
                if b + 1 < B:
                    transpose_xn(b + 1)
                    project(b + 1)
                transpose_probs(b)
                if b == 0:
                    pe.wait_ge(s_const, 3)
                    slot_counts(R2)
                    slot_table(R2)
                attend(b)
            pe.wait_ge(s_ctx, 16)
            pe.wait_ge(R2.s_ready, 1)
            expert_tensor(X2)

            def gate(t):
                if t == 0:
                    pe.wait_ge(s_gate, 16)
                pe.wait_ge(s_h3T_sb, t + 1)
                if t >= 2:
                    pe.wait_ge(s_idx8, t - 1)
                product(bank[2 + t % 2][:, 0:E3], [h3T_sb[:, t % 2, k, :] for k in range(KD)],
                        [gate_sb[:, k, :] for k in range(KD)], s_logit)

            for t in range(NT):
                pe.wait_ge(s_norm[3], t + 1)
                if t >= 2:
                    pe.wait_ge(s_h3T_sb, t - 1)
                for k in range(KD):
                    ins = pe.transpose(bank[t % 2][:, k * P:(k + 1) * P], cols(h3_sb[:, t, :], k), ident[:, :])
                ins.then_inc(s_h3T, 1)
                if t >= 1:
                    gate(t - 1)
            gate(NT - 1)
            slot_counts(R3)
            slot_table(R3)
            for s in (s_w13, s_w2a, s_w2b):
                pe.wait_ge(s, 16)
            pe.wait_ge(R3.s_ready, 1)
            expert_tensor(X3)


def build(nc, args):
    decoder_layer(nc, *args)


def kernel(**inputs):
    import concourse.bacc as _bacc
    from concourse import mybir as _mybir
    from concourse.bass_utils import run_bass_kernel_spmd as _run

    a = {k: np.asarray(v) for k, v in inputs.items()}
    x = a["x"]
    T, D = x.shape[0] * x.shape[1], x.shape[2]
    KD = D // P
    ctx, qkv, wo = a["ctx_2048"], a["L0_attn_qkv"], a["L0_attn_o_proj"]
    w1, w2, w3, gate = a["L0_ffn_w1"], a["L0_ffn_w2"], a["L0_ffn_w3"], a["L0_ffn_gate_w"]
    E2, E3 = ctx.shape[0], gate.shape[0]
    laid = {
        "x": x.reshape(T, D),
        "ids": a["itok_BxS_13_99985"],
        "ctx_t": ctx.reshape(E2, D, KD, P).transpose(3, 2, 0, 1),
        "qkv_t": qkv.reshape(D, 3, KD, P).transpose(3, 1, 2, 0),
        "wo": wo.reshape(KD, P, D).transpose(1, 0, 2),
        "gamma_beta": np.stack([a["L0_attn_gamma"], a["L0_attn_beta"]]).reshape(2, KD, P).transpose(2, 0, 1),
        "gate_t": gate.reshape(E3, KD, P).transpose(2, 1, 0),
        "w13_t": np.concatenate([w1, w3], axis=1).reshape(E3, -1, KD, P).transpose(3, 2, 0, 1),
        "w2_lo_t": w2[:, :, 0:P].transpose(2, 0, 1),
        "w2_hi_t": w2[:, :, P:].transpose(2, 0, 1),
    }
    nc = _bacc.Bacc("TRN2", target_bir_lowering=False, num_devices=1)
    arrays, args = {}, []
    for name, v in laid.items():
        v = np.ascontiguousarray(v)
        arrays[f"in_{name}"] = v
        args.append(nc.dram_tensor(f"in_{name}", v.shape, _mybir.dt.from_np(v.dtype), kind="ExternalInput").ap())
    args.append(nc.dram_tensor("out_rows", [T, D], _mybir.dt.float32, kind="ExternalOutput").ap())
    build(nc, args)
    r = _run(nc, [arrays], core_ids=[0])
    return r.results[0]["out_rows"].reshape(x.shape)
```

```python
from contextlib import ExitStack

import numpy as np

import concourse.bass as bass
from concourse import mybir

F32 = mybir.dt.float32
BF16 = mybir.dt.bfloat16
I32 = mybir.dt.int32
U32 = mybir.dt.uint32
ALU = mybir.AluOpType
ACT = mybir.ActivationFunctionType
AX = mybir.AxisListType

P = 128
EPS = 1e-5
MASKED = -1e30
ROUND = 1.5 * 2.0 ** 23


def decoder_layer(nc, x, ids, ctx_t, qkv_t, wo, gamma_beta, gate_t, w13_t, w2_lo_t, w2_hi_t, out):
    T, D = x.shape
    KD = D // P
    NT = T // P
    B = ids.shape[0]
    TB = NT // B
    S = T // B
    E2 = ctx_t.shape[2]
    VOCAB = 12500
    PER_EXPERT = VOCAB // E2
    E3 = gate_t.shape[2]
    TOPK = 2
    F3 = w13_t.shape[3] // 2
    F3R = F3 - P
    HALVES = 2
    BH = B // HALVES
    NT2H = T // P // HALVES + E2 - 1
    NT2 = HALVES * NT2H
    NT3 = TOPK * T // P + E3 - 1
    LOOP = 8
    FIRST = 6
    assert KD == 2 and TB == 2 and D == 256 and P < F3 <= 2 * P

    with ExitStack() as stack:
        def sb(name, shape, dt=F32):
            return stack.enter_context(nc.sbuf_tensor(name, shape, dt))

        def sem(name):
            return stack.enter_context(nc.semaphore(name))

        h2_dram = [nc.dram_tensor(f"h2_rows{h}", [T // HALVES, D], F32).ap() for h in range(HALVES)]
        y2_dram = nc.dram_tensor("y2_rows", [T + NT2 * P, D], F32).ap()
        h3_dram = nc.dram_tensor("h3_rows", [T, D], F32).ap()
        y3_dram = nc.dram_tensor("y3_rows", [TOPK * T + NT3 * P, D], F32).ap()

        bank = [stack.enter_context(nc.psum_tensor(f"bank{i}", [P, 512], F32)) for i in range(8)]

        ident = sb("ident", [P, P])
        ident_bf = sb("ident_bf", [P, P], BF16)
        causal_bf = sb("causal_bf", [P, S], BF16)
        before_bf = sb("before_bf", [P, P], BF16)
        ones_bf = sb("ones_bf", [P, P], BF16)
        iota_slot = sb("iota_slot", [P, P])
        iota_bf = sb("iota_bf", [P, P], BF16)
        iota_part = sb("iota_part", [P, 1])
        iota_col = sb("iota_col", [P, TOPK * NT])
        pow_half = sb("pow_half", [P, TB])

        qkv_sb = sb("qkv_sb", [P, 3, KD, D])
        wo_sb = sb("wo_sb", [P, KD, D])
        gb_sb = sb("gb_sb", [P, 2, KD])
        qk_sb = sb("qk_sb", [P, KD, D])
        vo_sb = sb("vo_sb", [P, KD, D])
        ctx_sb = sb("ctx_sb", [P, KD, E2, D])
        gate_sb = sb("gate_sb", [P, KD, E3])
        w13_sb = sb("w13_sb", [P, KD, E3, 2 * F3])
        w2a_sb = sb("w2a_sb", [P, E3, D])
        w2b_sb = sb("w2b_sb", [F3R, E3, D])

        x_sb = sb("x_sb", [P, NT, D])
        h1_sb = sb("h1_sb", [P, NT, D])
        xn_sb = sb("xn_sb", [P, NT, D])
        xh_sb = sb("xh_sb", [P, NT, D])
        x1_sb = sb("x1_sb", [P, NT, D])
        h2_sb = xn_sb
        x2_sb = x_sb
        h3_sb = h1_sb
        y2_sb = xh_sb
        y3_sb = sb("y3_sb", [P, TOPK, NT, D])
        out_sb = x1_sb

        NORMS = 4
        stats = sb("stats", [P, NORMS, NT, 6])
        meanvar = sb("meanvar", [P, NORMS, NT, 2])
        vareps = sb("vareps", [P, NORMS, NT])
        rstd = sb("rstd", [P, NORMS, NT])
        shift = sb("shift", [P, B])

        xnT_sb = sb("xnT_sb", [P, 2, KD, S])
        pT_sb = sb("pT_sb", [P, 2, KD, S])
        vv_sb = sb("vv_sb", [P, 2, TB, D])
        prob_sb = sb("prob_sb", [P, 2, TB, S])
        probT_sb = sb("probT_sb", [P, 2, 3, P])
        negmax = sb("negmax", [P, NT])
        rowsum = sb("rowsum", [P, NT])
        rowinv = sb("rowinv", [P, NT])

        class Routing:
            def __init__(self, tag, E, C, tiles):
                self.tag, self.E, self.C, self.tiles = tag, E, C, tiles
                self.expert = sb(f"{tag}_expert", [P, C])
                self.onehot = sb(f"{tag}_onehot", [P, E, C], BF16)
                self.goes_on = sb(f"{tag}_goes_on", [P, E, C])
                self.cum = sb(f"{tag}_cum", [P, E, C])
                self.rank = sb(f"{tag}_rank", [P, E, C])
                self.ntile_x = sb(f"{tag}_ntile_x", [P, E])
                self.ntile = sb(f"{tag}_ntile", [P, E])
                self.carry = sb(f"{tag}_carry", [P, E])
                self.end = sb(f"{tag}_end", [P, E])
                self.start = sb(f"{tag}_start", [P, E])
                self.slot = sb(f"{tag}_slot", [P, C])
                self.tile_x = sb(f"{tag}_tile_x", [P, C])
                self.tile_of = sb(f"{tag}_tile_of", [P, C])
                self.row_of = sb(f"{tag}_row_of", [P, C])
                self.at_row = sb(f"{tag}_at_row", [P, C, P], BF16)
                self.at_tile = sb(f"{tag}_at_tile", [P, C, 3, tiles], BF16)
                self.table = sb(f"{tag}_table", [P, 3, tiles])
                self.spare = sb(f"{tag}_spare", [P, tiles])
                self.unused = sb(f"{tag}_unused", [P, tiles])
                self.dest_f = sb(f"{tag}_dest_f", [P, tiles])
                self.dest = sb(f"{tag}_dest", [P, tiles], I32)
                self.src = sb(f"{tag}_src", [P, tiles], I32)
                self.past = sb(f"{tag}_past", [P, tiles, E])
                self.tile_f = sb(f"{tag}_tile_f", [P, tiles])
                self.tile_expert = sb(f"{tag}_tile_expert", [P, tiles], I32)
                self.s_onehot = sem(f"{tag}_s_onehot")
                self.s_counts = sem(f"{tag}_s_counts")
                self.s_step = sem(f"{tag}_s_step")
                self.s_init = sem(f"{tag}_s_init")
                self.s_rows = sem(f"{tag}_s_rows")
                self.s_table = sem(f"{tag}_s_table")
                self.s_ready = sem(f"{tag}_s_ready")

        R2 = Routing("r2", HALVES * E2, NT, NT2)
        half_first = sb("half_first", [P, NT])
        half_offset = sb("half_offset", [P, HALVES * E2])
        half_counted = sb("half_counted", [P, NT2])
        half_last = sb("half_last", [P, NT2])
        ntile_offset = sb("ntile_offset", [P, HALVES * E2])
        R3 = Routing("r3", E3, TOPK * NT, NT3)
        R2.psum, R2.psum_table = bank[7], bank[7][:, 64:64 + 3 * NT2]
        R2.rows, R3.rows = T // HALVES, T
        R3.psum, R3.psum_table = bank[4], bank[5][:, 0:3 * NT3]
        ids_sb = sb("ids_sb", [NT, P], I32)
        ids_f = sb("ids_f", [NT, P])
        top_val = sb("top_val", [P, NT, 8])
        top_idx = sb("top_idx", [P, NT, 8], U32)
        gap = sb("gap", [P, NT])
        top_w = sb("top_w", [P, TOPK, NT])
        h3T_sb = sb("h3T_sb", [P, 2, KD, P])

        rows_in = sb("rows_in", [P, 4, D])
        rowsT = sb("rowsT", [P, 2, KD, P])
        silu_sb = sb("silu_sb", [P, 2, D])
        prod_sb = sb("prod_sb", [P, 2, D])
        prodT = sb("prodT", [P, 2, 2, P])
        rows_out = sb("rows_out", [P, 4, D])

        s_ids = sem("s_ids")
        s_x = [sem(f"s_x_in{b}") for b in range(B)]
        s_wattn = sem("s_wattn")
        s_wv = sem("s_wv")
        s_wo = sem("s_wo")
        s_gb = sem("s_gb")
        s_ctx = sem("s_ctx")
        s_gate = sem("s_gate")
        s_w13 = sem("s_w13")
        s_w2a = sem("s_w2a")
        s_w2b = sem("s_w2b")
        s_fill = sem("s_fill")
        s_ident = sem("s_ident")
        s_const = sem("s_const")
        s_qk = sem("s_qk")
        s_vo = sem("s_vo")
        s_qk_sb = sem("s_qk_sb")
        s_vo_sb = sem("s_vo_sb")
        s_stat = [sem(f"s_stat{n}") for n in range(NORMS)]
        s_mv = [sem(f"s_mv{n}") for n in range(NORMS)]
        s_var = [sem(f"s_var{n}") for n in range(NORMS)]
        s_rstd = [sem(f"s_rstd{n}") for n in range(NORMS)]
        s_norm = [sem(f"s_norm{n}") for n in range(NORMS)]
        s_xh = sem("s_xh")
        s_xnT = sem("s_xnT")
        s_xnT_sb = sem("s_xnT_sb")
        s_pT = sem("s_pT")
        s_pT_sb = sem("s_pT_sb")
        s_vv = sem("s_vv")
        s_vv_sb = sem("s_vv_sb")
        s_score = sem("s_score")
        s_max = sem("s_max")
        s_exp = sem("s_exp")
        s_probT = sem("s_probT")
        s_probT_sb = sem("s_probT_sb")
        s_inv = sem("s_inv")
        s_attn = sem("s_attn")
        s_x1 = sem("s_x1")
        s_h2_out = [sem(f"s_h2_out{b}") for b in range(B)]
        s_y2_in = [sem(f"s_y2_in{b}") for b in range(B)]
        s_x2 = sem("s_x2")
        s_shift = sem("s_shift")
        s_norm3_act = sem("s_norm3_act")
        s_h3_out = sem("s_h3_out")
        s_h3T = sem("s_h3T")
        s_h3T_sb = sem("s_h3T_sb")
        s_logit = sem("s_logit")
        s_max8 = sem("s_max8")
        s_idx8 = sem("s_idx8")
        s_gap = sem("s_gap")
        s_topw = sem("s_topw")
        s_idsf = sem("s_idsf")
        s_idsT = sem("s_idsT")
        s_y3_in = [sem(f"s_y3_in{b}") for b in range(B)]
        s_mix = sem("s_mix")
        s_sum = sem("s_sum")
        s_out = sem("s_out")

        class ExpertBlock:
            def __init__(self, tag, routing, first_w, first_n, width, second_w, src, dst):
                self.routing, self.tiles = routing, routing.tiles
                self.first_w, self.first_n, self.width = first_w, first_n, width
                self.second_w, self.src, self.dst = second_w, src, dst
                self.s_in = [sem(f"{tag}_in{m}") for m in range(4)]
                self.s_rowsT = sem(f"{tag}_rowsT")
                self.s_rowsT_sb = sem(f"{tag}_rowsT_sb")
                self.s_first = sem(f"{tag}_first")
                self.s_silu = sem(f"{tag}_silu")
                self.s_prod = sem(f"{tag}_prod")
                self.s_prodT = sem(f"{tag}_prodT")
                self.s_prodT_sb = sem(f"{tag}_prodT_sb")
                self.s_rest_sb = sem(f"{tag}_rest_sb")
                self.s_second = sem(f"{tag}_second")
                self.s_y = sem(f"{tag}_y")
                self.s_done = [sem(f"{tag}_done{m}") for m in range(4)]

            def scattered(self, eng, tiles):
                for m in range(4):
                    eng.wait_ge(self.s_done[m], 16 * len(range(m, tiles, 4)))

        X2 = ExpertBlock("x2", R2, ctx_sb, D, D, [ctx_sb[:, k] for k in range(KD)], h2_dram, y2_dram)
        X3 = ExpertBlock("x3", R3, w13_sb, 2 * F3, F3, [w2a_sb, w2b_sb], [h3_dram], y3_dram)

        def pipeline(eng, tiles, step, turn=lambda: None):
            def at(i):
                step(i, i % 4, i // 4, i)
            turns = (tiles - 1 - FIRST) // LOOP
            if turns < 2:
                turns = 0
            for i in range(FIRST):
                at(i)
            if turns:
                with nc.Fori(0, turns, engines=(eng.engine,), hint_back_edge=True) as n:
                    turn()
                    for u in range(FIRST, FIRST + LOOP):
                        step(n * LOOP + u, u % 4, n * (LOOP // 4) + u // 4, None)
            turn()
            for i in range(FIRST + LOOP * turns, tiles + 2):
                at(i)

        block = stack.enter_context(nc.Block())

        @block.sync
        def _(sp):
            rows = x.rearrange("(c p) d -> p c d", p=P)
            for b in range(B):
                sp.dma_start(x_sb[:, b * TB:(b + 1) * TB, :], rows[:, b * TB:(b + 1) * TB, :]).then_inc(s_x[b], 16)
            sp.dma_start(ctx_sb[:, :, :, :], ctx_t).then_inc(s_ctx, 16)
            sp.dma_start(gate_sb[:, :, :], gate_t).then_inc(s_gate, 16)
            sp.dma_start(w13_sb[:, :, :, :], w13_t).then_inc(s_w13, 16)
            sp.dma_start(w2a_sb[:, :, :], w2_lo_t).then_inc(s_w2a, 16)
            sp.dma_start(w2b_sb[:, :, :], w2_hi_t).then_inc(s_w2b, 16)
            h3_rows = h3_dram.rearrange("(c p) d -> p c d", p=P)
            for b in range(B):
                sp.wait_ge(s_norm[2], TB * (b + 1))
                h2_rows = h2_dram[b // BH].rearrange("(c p) d -> p c d", p=P)
                sp.dma_start(h2_rows[:, b % BH * TB:(b % BH + 1) * TB, :], h2_sb[:, b * TB:(b + 1) * TB, :]).then_inc(s_h2_out[b], 16)
            y2_rows = y2_dram[0:T, :].rearrange("(c p) d -> p c d", p=P)
            for b in range(B):
                if b % BH == 0:
                    X2.scattered(sp, NT2H * (b // BH + 1))
                sp.dma_start(y2_sb[:, b * TB:(b + 1) * TB, :], y2_rows[:, b * TB:(b + 1) * TB, :]).then_inc(s_y2_in[b], 16)
            for b in range(B):
                sp.wait_ge(s_norm[3], b + 1)
                sp.wait_ge(s_norm3_act, b + 1)
                sp.dma_start(h3_rows[:, b * TB:(b + 1) * TB, :], h3_sb[:, b * TB:(b + 1) * TB, :]).then_inc(s_h3_out, 16)
            X3.scattered(sp, NT3)
            y3_rows = y3_dram[0:TOPK * T, :].rearrange("(k c p) d -> p k c d", k=TOPK, p=P)
            for b in range(B):
                for k in range(TOPK):
                    sp.dma_start(y3_sb[:, k, b * TB:(b + 1) * TB, :], y3_rows[:, k, b * TB:(b + 1) * TB, :]).then_inc(s_y3_in[b], 16)
            out_rows = out.rearrange("(c p) d -> p c d", p=P)
            for b in range(B):
                sp.wait_ge(s_sum, TB * (b + 1))
                sp.dma_start(out_rows[:, b * TB:(b + 1) * TB, :], out_sb[:, b * TB:(b + 1) * TB, :]).then_inc(s_out, 16)
            sp.wait_ge(s_out, 16 * B)

        @block.gpsimd
        def _(pool):
            pool.memset(ident[:, :], 0.0).then_inc(s_fill, 1)
            pool.memset(pow_half[:, :], -0.5).then_inc(s_fill, 1)
            pool.wait_ge(s_fill, 1)
            pool.affine_select(out=ident[:, :], in_=ident[:, :], compare_op=ALU.not_equal, fill=1.0, base=0,
                               pattern=[[-1, P]], channel_multiplier=1).then_inc(s_ident, 1)
            pool.memset(causal_bf[:, :], 0.0).then_inc(s_fill, 1)
            pool.memset(before_bf[:, :], 1.0).then_inc(s_fill, 1)
            pool.memset(ones_bf[:, :], 1.0).then_inc(s_fill, 1)
            pool.wait_ge(s_ident, 1)
            pool.tensor_copy(ident_bf[:, :], ident[:, :]).then_inc(s_const, 1)
            pool.wait_ge(s_fill, 5)
            pool.affine_select(out=causal_bf[:, :], in_=causal_bf[:, :], compare_op=ALU.is_ge, fill=MASKED, base=S - P,
                               pattern=[[-1, S]], channel_multiplier=1).then_inc(s_const, 1)
            pool.affine_select(out=before_bf[:, :], in_=before_bf[:, :], compare_op=ALU.is_gt, fill=0.0, base=0,
                               pattern=[[1, P]], channel_multiplier=-1).then_inc(s_const, 1)
            pool.iota(iota_slot[:, :], pattern=[[1, P]], base=0, channel_multiplier=0,
                      allow_small_or_imprecise_dtypes=True).then_inc(s_const, 1)
            pool.iota(iota_part[:, :], pattern=[[0, 1]], base=0, channel_multiplier=1,
                      allow_small_or_imprecise_dtypes=True).then_inc(s_const, 1)
            pool.iota(iota_col[:, :], pattern=[[1, TOPK * NT]], base=0, channel_multiplier=0,
                      allow_small_or_imprecise_dtypes=True).then_inc(s_const, 1)

            pool.iota(iota_bf[:, :], pattern=[[1, P]], base=0, channel_multiplier=0,
                      allow_small_or_imprecise_dtypes=True).then_inc(s_const, 1)
            for R in (R2, R3):
                pool.iota(R.spare[:, :], pattern=[[P, R.tiles]], base=R.C * P, channel_multiplier=1,
                          allow_small_or_imprecise_dtypes=True).then_inc(s_const, 1)

            def inverse_root(n, b):
                pool.wait_ge(s_var[n], b + 1)
                pool.tensor_tensor(rstd[:, n, b * TB:(b + 1) * TB], vareps[:, n, b * TB:(b + 1) * TB], pow_half[:, :],
                                   ALU.pow).then_inc(s_rstd[n], 1)

            def residual(b):
                pool.wait_ge(s_norm[0], TB * (b + 1))
                pool.tensor_tensor(xh_sb[:, b * TB:(b + 1) * TB, :], x_sb[:, b * TB:(b + 1) * TB, :],
                                   h1_sb[:, b * TB:(b + 1) * TB, :], ALU.add).then_inc(s_xh, 1)

            def half_ready(j):
                if j % NT2H == 0:
                    for b in range(BH):
                        pool.wait_ge(s_h2_out[j // NT2H * BH + b], 16)

            def route_by_slot(blk, start, ready=None, between=lambda j: None):
                def gather(j):
                    if ready is not None:
                        ready(j)
                    if j >= 4:
                        pool.wait_ge(blk.s_rowsT, j - 3)
                    pool.indirect_dma_start(
                        out=rows_in[:, j % 4, :], out_offset=None, in_=blk.src[j * len(blk.src) // blk.tiles],
                        in_offset=bass.IndirectOffsetOnAxis(ap=blk.routing.src[:, j:j + 1].bitcast(U32), axis=0),
                    ).then_inc(blk.s_in[j % 4], 16)

                def scatter(j):
                    pool.wait_ge(blk.s_y, j + 1)
                    pool.indirect_dma_start(
                        out=blk.dst, in_=rows_out[:, j % 4, :], in_offset=None,
                        out_offset=bass.IndirectOffsetOnAxis(ap=blk.routing.dest[:, j:j + 1].bitcast(U32), axis=0),
                    ).then_inc(blk.s_done[j % 4], 16)

                if start:
                    for j in range(4):
                        gather(j)
                    return
                LAG = 3
                for j in range(blk.tiles + LAG):
                    if j + 4 < blk.tiles:
                        gather(j + 4)
                    if j >= LAG:
                        scatter(j - LAG)
                    between(j - LAG)

            inverse_root(0, 0)
            inverse_root(0, 1)
            inverse_root(1, 0)
            inverse_root(0, 2)
            inverse_root(1, 1)
            residual(0)
            inverse_root(1, 2)
            residual(1)
            residual(2)
            for b in range(B):
                if b >= 1:
                    inverse_root(2, b - 1)
                if b + 3 < B:
                    inverse_root(0, b + 3)
                    inverse_root(1, b + 3)
                    residual(b + 3)
            pool.wait_ge(R2.s_ready, 1)
            route_by_slot(X2, True, half_ready)
            inverse_root(2, B - 1)
            def first_half_roots(j):
                if NT2 - 3 <= j < NT2 - 3 + BH:
                    inverse_root(3, j - (NT2 - 3))
            route_by_slot(X2, False, half_ready, first_half_roots)
            for b in range(BH, B):
                inverse_root(3, b)
            pool.wait_ge(s_h3_out, 16 * B)
            pool.wait_ge(R3.s_ready, 1)
            route_by_slot(X3, True)
            route_by_slot(X3, False)

        @block.vector
        def _(dve):
            for R in (R2, R3):
                dve.memset(R.carry[:, :], 1.0).then_inc(R.s_init, 1)
                dve.memset(R.goes_on[:, :, :], 1.0).then_inc(R.s_init, 1)
            dve.memset(half_first[:, :], 0.0).then_inc(R2.s_init, 1)
            dve.memset(half_offset[:, :], 0.0).then_inc(R2.s_init, 1)
            dve.memset(half_counted[:, :], 0.0).then_inc(R2.s_init, 1)
            dve.memset(half_last[:, :], float(E2 - 1)).then_inc(R2.s_init, 1)
            for R in (R2, R3):
                dve.wait_ge(R.s_init, 2)
                dve.memset(R.goes_on[:, :, 0:1], 0.0).then_inc(R.s_init, 1)
            dve.wait_ge(R2.s_init, 6)
            dve.memset(R2.carry[:, E2:E2 + 1], 0.0).then_inc(R2.s_init, 1)
            dve.memset(half_first[:, NT // 2:NT], float(E2)).then_inc(R2.s_init, 1)
            dve.memset(half_offset[:, E2:E2 + 1], float(NT2H)).then_inc(R2.s_init, 1)
            dve.memset(half_counted[:, NT2H:NT2], float(E2)).then_inc(R2.s_init, 1)
            dve.memset(half_last[:, NT2H:NT2], float(2 * E2 - 1)).then_inc(R2.s_init, 1)

            def moments(n, src, b):
                ts = range(b * TB, (b + 1) * TB)
                for t in ts:
                    dve.bn_stats(stats[:, n, t, :], src[:, t, :]).then_inc(s_stat[n], 1)
                for t in ts:
                    dve.wait_ge(s_stat[n], t + 1)
                    dve.bn_aggr(meanvar[:, n, t, :], stats[:, n, t, :]).then_inc(s_mv[n], 1)
                dve.wait_ge(s_mv[n], TB * (b + 1))
                dve.tensor_scalar(vareps[:, n, b * TB:(b + 1) * TB], meanvar[:, n, b * TB:(b + 1) * TB, 1], EPS, None,
                                  ALU.add).then_inc(s_var[n], 1)

            def normalise(n, dst, src, b):
                dve.wait_ge(s_rstd[n], b + 1)
                for t in range(b * TB, (b + 1) * TB):
                    dve.tensor_scalar(dst[:, t, :], src[:, t, :], meanvar[:, n, t, 0:1], rstd[:, n, t:t + 1],
                                      ALU.subtract, ALU.mult).then_inc(s_norm[n], 1)

            def norm_a(b):
                dve.wait_ge(s_x[b], 16)
                moments(0, x_sb, b)

            def norm_b(b):
                normalise(0, h1_sb, x_sb, b)
                dve.wait_ge(s_norm[0], TB * (b + 1))
                moments(1, h1_sb, b)

            def norm_c(b):
                normalise(1, xn_sb, h1_sb, b)

            def row_max(b):
                for i in range(TB):
                    t = b * TB + i
                    dve.wait_ge(s_score, t + 1)
                    dve.tensor_reduce(negmax[:, t:t + 1], bank[3 + i][:, 0:(i + 1) * P], AX.X, ALU.max,
                                      negate=True).then_inc(s_max, 1)

            def prob_transposed(b):
                dve.wait_ge(s_probT, b + 1)
                if b >= 2:
                    dve.wait_ge(s_attn, b - 1)
                dve.tensor_copy(probT_sb[:, b % 2, :, :], bank[5][:, 0:3 * P]).then_inc(s_probT_sb, 1)
                dve.wait_ge(s_exp, TB * (b + 1))
                dve.reciprocal(rowinv[:, b * TB:(b + 1) * TB], rowsum[:, b * TB:(b + 1) * TB]).then_inc(s_inv, 1)

            def attention_out(b):
                dve.wait_ge(s_attn, b + 1)
                dve.wait_ge(s_inv, b + 1)
                dve.wait_ge(s_xh, b + 1)
                for i in range(TB):
                    t = b * TB + i
                    dve.scalar_tensor_tensor(out=x1_sb[:, t, :], in0=bank[6][:, i * D:(i + 1) * D],
                                             scalar=rowinv[:, t:t + 1], in1=xh_sb[:, t, :], op0=ALU.mult,
                                             op1=ALU.add).then_inc(s_x1, 1)
                dve.wait_ge(s_x1, TB * (b + 1))
                moments(2, x1_sb, b)

            def token_experts():
                dve.wait_ge(s_idsT, 1)
                dve.wait_ge(R2.s_init, 12)
                for e in range(1, E2):
                    if e > 1:
                        dve.wait_ge(R2.s_step, e - 1)
                    dve.scalar_tensor_tensor(out=R2.expert[:, :], in0=bank[7][:, 0:NT], scalar=float(e * PER_EXPERT),
                                             in1=half_first[:, :] if e == 1 else R2.expert[:, :],
                                             op0=ALU.is_ge, op1=ALU.add).then_inc(R2.s_step, 1)
                dve.wait_ge(R2.s_step, E2 - 1)

            class Steps:
                def __init__(self, R, done):
                    self.R, self.n = R, done

                def step(self, ins):
                    self.n += 1
                    ins.then_inc(self.R.s_step, 1)

                def join(self):
                    dve.wait_ge(self.R.s_step, self.n)

            def slot_onehot(R):
                E, C = R.E, R.C
                dve.tensor_tensor(R.onehot[:, :, :], iota_slot[:, 0:E].rearrange("p (e o) -> p e o", o=1).to_broadcast([P, E, C]),
                                  R.expert[:, :].rearrange("p (o c) -> p o c", o=1).to_broadcast([P, E, C]),
                                  ALU.is_equal).then_inc(R.s_onehot, 1)

            def slot_ranks(R, done):
                own = Steps(R, done)
                step, join = own.step, own.join
                E, C, NTL = R.E, R.C, R.tiles
                dve.wait_ge(R.s_counts, 1)
                in_tile = R.psum[:, 0:E * C]
                totals = R.psum[:, 256:256 + E * C]
                flat = lambda a: a[:, :, :].rearrange("p e c -> p (e c)")
                step(dve.tensor_tensor_scan(flat(R.cum), flat(R.goes_on), totals, 0.0, ALU.mult, ALU.add))
                join()
                step(dve.tensor_tensor(flat(R.rank), flat(R.cum), totals, ALU.subtract))
                step(dve.tensor_scalar(R.ntile_x[:, :], R.cum[:, :, C - 1], 1.0 / P, (P - 1) / (2.0 * P), ALU.mult, ALU.add))
                join()
                step(dve.tensor_tensor(flat(R.rank), flat(R.rank), in_tile, ALU.add))
                step(dve.tensor_scalar(R.ntile[:, :], R.ntile_x[:, :], ROUND, -ROUND, ALU.add, ALU.add))
                join()
                widths = R.ntile
                if R is R2:
                    widths = ntile_offset
                    step(dve.tensor_tensor(widths[:, :], R.ntile[:, :], half_offset[:, :], ALU.add))
                    join()
                step(dve.tensor_tensor_scan(R.end[:, :], R.carry[:, :], widths[:, :], 0.0, ALU.mult, ALU.add))
                join()
                step(dve.tensor_tensor(R.start[:, :], R.end[:, :], R.ntile[:, :], ALU.subtract))
                step(dve.tensor_tensor(R.past[:, :, :],
                                       iota_slot[:, 0:NTL].rearrange("p (j o) -> p j o", o=1).to_broadcast([P, NTL, E]),
                                       R.end[:, :].rearrange("p (o e) -> p o e", o=1).to_broadcast([P, NTL, E]), ALU.is_ge))
                join()
                step(dve.scalar_tensor_tensor(out=R.rank[:, :, :],
                                              in0=R.start[:, :].rearrange("p (e o) -> p e o", o=1).to_broadcast([P, E, C]),
                                              scalar=float(P), in1=R.rank[:, :, :], op0=ALU.mult, op1=ALU.add))
                step(dve.tensor_reduce(R.tile_f[:, :], R.past[:, :, :], AX.X, ALU.add))
                join()
                step(dve.tensor_tensor(R.rank[:, :, :], R.rank[:, :, :], R.onehot[:, :, :], ALU.mult))
                if R is R2:
                    step(dve.tensor_tensor(R.tile_f[:, :], R.tile_f[:, :], half_last[:, :], ALU.min))
                    join()
                    step(dve.tensor_tensor(R.tile_expert[:, :], R.tile_f[:, :], half_counted[:, :], ALU.subtract))
                else:
                    step(dve.tensor_scalar(R.tile_expert[:, :], R.tile_f[:, :], float(E - 1), None, ALU.min))
                    join()
                step(dve.tensor_reduce(R.slot[:, :], R.rank[:, :, :].rearrange("p e c -> p c e"), AX.X, ALU.add))
                join()
                step(dve.tensor_scalar(R.tile_x[:, :], R.slot[:, :], 1.0 / P, -(P - 1) / (2.0 * P), ALU.mult, ALU.add))
                return own.n

            def slot_rows(R, done):
                own = Steps(R, done)
                step, join = own.step, own.join
                C, NTL = R.C, R.tiles
                join()
                step(dve.tensor_scalar(R.tile_of[:, :], R.tile_x[:, :], ROUND, -ROUND, ALU.add, ALU.add))
                join()
                step(dve.tensor_tensor(R.at_tile[:, :, 2, :],
                                       iota_slot[:, 0:NTL].rearrange("p (o j) -> p o j", o=1).to_broadcast([P, C, NTL]),
                                       R.tile_of[:, :].rearrange("p (c o) -> p c o", o=1).to_broadcast([P, C, NTL]),
                                       ALU.is_equal))
                step(dve.scalar_tensor_tensor(out=R.row_of[:, :], in0=R.tile_of[:, :], scalar=float(-P), in1=R.slot[:, :],
                                              op0=ALU.mult, op1=ALU.add))
                join()
                step(dve.tensor_scalar(R.at_tile[:, :, 0, :], R.at_tile[:, :, 2, :], iota_part[:, 0:1], None, ALU.mult))
                step(dve.tensor_tensor(R.at_tile[:, :, 1, :], R.at_tile[:, :, 2, :],
                                       iota_col[:, 0:C].rearrange("p (c o) -> p c o", o=1).to_broadcast([P, C, NTL]),
                                       ALU.mult))
                for c in range(C):
                    dve.tensor_scalar(R.at_row[:, c, :], iota_bf[:, :], R.row_of[:, c:c + 1], None,
                                      ALU.is_equal).then_inc(R.s_rows, 1)
                return own.n

            def slot_tables(R, done):
                own = Steps(R, done)
                step, join = own.step, own.join
                dve.wait_ge(R.s_table, 1)
                step(dve.tensor_copy(R.table[:, :, :], R.psum_table))
                join()
                step(dve.scalar_tensor_tensor(out=R.dest_f[:, :], in0=R.table[:, 1, :], scalar=float(P),
                                              in1=R.table[:, 0, :], op0=ALU.mult, op1=ALU.add))
                step(dve.scalar_tensor_tensor(out=R.unused[:, :], in0=R.table[:, 2, :], scalar=0.0, in1=R.spare[:, :],
                                              op0=ALU.is_equal, op1=ALU.mult))
                join()
                step(dve.tensor_tensor(R.dest[:, :], R.dest_f[:, :], R.unused[:, :], ALU.add))
                join()
                dve.tensor_scalar(R.src[:, :], R.dest[:, :], R.rows - 1, None, ALU.bitwise_and).then_inc(R.s_ready, 1)

            def expert_vector(blk, after=lambda i: None):
                factor0 = blk.first_n - blk.width

                def step(i, m, q, known):
                    def rows_transposed(j, mj):
                        dve.wait_ge(blk.s_rowsT, j + 1)
                        if known is None or known >= 1:
                            dve.wait_ge(blk.s_first, j - 1)
                        dve.tensor_copy(rowsT[:, mj % 2, :, :], bank[mj % 2][:, 0:D]).then_inc(blk.s_rowsT_sb, 1)

                    if known == 0:
                        dve.wait_ge(blk.s_rowsT, 1)
                        dve.tensor_copy(rowsT[:, 0, :, :], bank[0][:, 0:D]).then_inc(blk.s_rowsT_sb, 1)
                    if known is None or known + 1 < blk.tiles:
                        rows_transposed(i + 1, m + 1)
                    if blk is X3 and (known is None or 2 <= known):
                        dve.wait_ge(blk.s_prodT, i - 1)
                        if known is None or known >= 4:
                            dve.wait_ge(blk.s_second, i - 3)
                        dve.tensor_copy(prodT[0:F3R, m % 2, 1, :], bank[m % 2][0:F3R, D:D + P]).then_inc(blk.s_rest_sb, 1)
                    if known is None or known < blk.tiles:
                        dve.wait_ge(blk.s_silu, i + 1)
                        if known is None or known >= 2:
                            dve.wait_ge(blk.s_prodT, i - 1)
                        dve.tensor_tensor(prod_sb[:, m % 2, 0:blk.width], silu_sb[:, m % 2, 0:blk.width],
                                          bank[2 + m % 2][:, factor0:factor0 + blk.width], ALU.mult).then_inc(blk.s_prod, 1)
                    after(known)
                pipeline(dve, blk.tiles, step)

            norm_a(0)
            norm_a(1)
            norm_b(0)
            dve.wait_ge(s_ids, 16)
            dve.tensor_copy(ids_f[:, :], ids_sb[:, :]).then_inc(s_idsf, 1)
            norm_a(2)
            norm_b(1)
            norm_c(0)
            token_experts()
            dve.wait_ge(s_const, 9)
            slot_onehot(R2)
            norm_b(2)
            norm_c(1)
            n = slot_ranks(R2, E2 - 1)
            for b in range(B):
                row_max(b)
                if b >= 1:
                    attention_out(b - 1)
                if b + 2 < B:
                    norm_c(b + 2)
                prob_transposed(b)
                if b + 3 < B:
                    norm_a(b + 3)
                    n = slot_rows(R2, n)
                if b >= 1:
                    normalise(2, h2_sb, x1_sb, b - 1)
                if b == 1:
                    slot_tables(R2, n)
                if b + 3 < B:
                    norm_b(b + 3)
            attention_out(B - 1)
            normalise(2, h2_sb, x1_sb, B - 1)

            def second_residual(b):
                dve.wait_ge(s_y2_in[b], 16)
                dve.tensor_tensor(x2_sb[:, b * TB:(b + 1) * TB, :], x1_sb[:, b * TB:(b + 1) * TB, :],
                                  y2_sb[:, b * TB:(b + 1) * TB, :], ALU.add).then_inc(s_x2, 1)
                dve.wait_ge(s_x2, b + 1)
                moments(3, x2_sb, b)

            def second_norm(b):
                t = b * TB
                dve.wait_ge(s_rstd[3], b + 1)
                dve.scalar_tensor_tensor(out=shift[:, b:b + 1], in0=meanvar[:, 3, t + 1, 0:1], scalar=-1.0,
                                         in1=rstd[:, 3, t + 1:t + 2], op0=ALU.mult, op1=ALU.mult).then_inc(s_shift, 1)
                dve.tensor_scalar(h3_sb[:, t, :], x2_sb[:, t, :], meanvar[:, 3, t, 0:1], rstd[:, 3, t:t + 1],
                                  ALU.subtract, ALU.mult).then_inc(s_norm[3], 1)

            def best_two(t):
                dve.wait_ge(s_logit, t + 1)
                lg = bank[2 + t % 2][:, 0:E3]
                dve.max(top_val[:, t, :], lg).then_inc(s_max8, 1)
                dve.wait_ge(s_max8, t + 1)
                dve.max_index(top_idx[:, t, :], top_val[:, t, :], lg).then_inc(s_idx8, 1)

            def first_half(i):
                n = i - (NT2 - 2)
                if 0 <= n < BH:
                    second_residual(n)
                if BH <= n < 2 * BH:
                    second_norm(n - BH)
            expert_vector(X2, first_half)
            for t in range(NT // 2):
                best_two(t)
            for b in range(BH, B):
                second_residual(b)
            for b in range(BH, B):
                second_norm(b)
            for t in range(NT // 2, NT):
                best_two(t)
            dve.wait_ge(s_idx8, NT)
            dve.tensor_copy(R3.expert[:, :].rearrange("p (k t) -> p t k", k=TOPK), top_idx[:, :, 0:TOPK]).then_inc(R3.s_step, 1)
            dve.tensor_tensor(gap[:, :], top_val[:, :, 0], top_val[:, :, 1], ALU.subtract).then_inc(s_gap, 1)
            dve.wait_ge(R3.s_init, 3)
            dve.wait_ge(R3.s_step, 1)
            slot_onehot(R3)
            slot_tables(R3, slot_rows(R3, slot_ranks(R3, 1)))
            expert_vector(X3)

            for b in range(B):
                ts = range(b * TB, (b + 1) * TB)
                dve.wait_ge(s_y3_in[b], 16 * TOPK)
                if b == 0:
                    dve.wait_ge(s_topw, TOPK)
                for t in ts:
                    dve.scalar_tensor_tensor(out=out_sb[:, t, :], in0=y3_sb[:, 0, t, :], scalar=top_w[:, 0, t:t + 1],
                                             in1=x2_sb[:, t, :], op0=ALU.mult, op1=ALU.add).then_inc(s_mix, 1)
                for t in ts:
                    dve.wait_ge(s_mix, t + 1)
                    dve.scalar_tensor_tensor(out=out_sb[:, t, :], in0=y3_sb[:, 1, t, :], scalar=top_w[:, 1, t:t + 1],
                                             in1=out_sb[:, t, :], op0=ALU.mult, op1=ALU.add).then_inc(s_sum, 1)

        @block.scalar
        def _(act):
            act.dma_start(qkv_sb[:, 0:2, :, :], qkv_t[:, 0:2, :, :]).then_inc(s_wattn, 16)
            act.dma_start(ids_sb[:, :], ids.rearrange("b (c p) -> (b c) p", p=P)).then_inc(s_ids, 16)
            act.dma_start(gb_sb[:, :, :], gamma_beta).then_inc(s_gb, 16)
            act.dma_start(qkv_sb[:, 2, :, :], qkv_t[:, 2, :, :]).then_inc(s_wv, 16)
            act.dma_start(wo_sb[:, :, :], wo).then_inc(s_wo, 16)
            act.wait_ge(s_qk, 1)
            act.activation(qk_sb[:, :, :], bank[3][:, :], ACT.Copy).then_inc(s_qk_sb, 1)

            def xn_transposed(b):
                act.wait_ge(s_xnT, b + 1)
                if b == 0:
                    act.wait_ge(s_gb, 16)
                if b >= 2:
                    act.wait_ge(s_score, TB * (b - 1))
                for k in range(KD):
                    act.activation(xnT_sb[:, b % 2, k, :], bank[0][:, k * S:(k + 1) * S], ACT.Identity,
                                   bias=gb_sb[:, 1, k:k + 1], scale=gb_sb[:, 0, k:k + 1]).then_inc(s_xnT_sb, 1)

            def projected_keys(b):
                act.wait_ge(s_pT, b + 1)
                if b >= 2:
                    act.wait_ge(s_score, TB * (b - 1))
                act.activation(pT_sb[:, b % 2, :, :], bank[1][:, :], ACT.Copy, scale=float(D) ** -0.5).then_inc(s_pT_sb, 1)

            def projected_values(b):
                act.wait_ge(s_vv, b + 1)
                if b >= 2:
                    act.wait_ge(s_attn, b - 1)
                act.activation(vv_sb[:, b % 2, :, :], bank[2][:, :], ACT.Copy).then_inc(s_vv_sb, 1)

            def exponentials(b):
                for i in range(TB):
                    t = b * TB + i
                    act.wait_ge(s_max, t + 1)
                    if b >= 2 and i == 0:
                        act.wait_ge(s_probT, b - 1)
                    act.activation(prob_sb[:, b % 2, i, 0:(i + 1) * P], bank[3 + i][:, 0:(i + 1) * P],
                                   ACT.Exp, bias=negmax[:, t:t + 1], accum_out=rowsum[:, t:t + 1]).then_inc(s_exp, 1)

            xn_transposed(0)
            act.wait_ge(s_vo, 1)
            act.activation(vo_sb[:, :, :], bank[4][:, :], ACT.Copy).then_inc(s_vo_sb, 1)
            projected_keys(0)
            xn_transposed(1)
            projected_values(0)
            for b in range(B):
                exponentials(b)
                if b + 1 < B:
                    projected_keys(b + 1)
                    if b + 2 < B:
                        xn_transposed(b + 2)
                    projected_values(b + 1)

            def expert_scalar(blk):
                def step(i, m, q, known):
                    if known is None or known >= 2:
                        act.wait_ge(blk.s_prodT, i - 1)
                        if known is None or known >= 4:
                            act.wait_ge(blk.s_second, i - 3)
                        n = D if blk is X2 else P
                        act.activation(prodT[:, m % 2, 0:n // P, :], bank[4 + m % 2][:, 0:n], ACT.Copy).then_inc(blk.s_prodT_sb, 1)
                    if known is None or known < blk.tiles:
                        act.wait_ge(blk.s_first, i + 1)
                        if known is None or known >= 2:
                            act.wait_ge(blk.s_prod, i - 1)
                        act.activation(silu_sb[:, m % 2, 0:blk.width], bank[2 + m % 2][:, 0:blk.width], ACT.Silu).then_inc(blk.s_silu, 1)
                    if known is None or known >= 2:
                        act.wait_ge(blk.s_second, i - 1)
                        if known is None or known >= 6:
                            act.wait_ge(blk.s_done[(m + 2) % 4], (q - (1 if m < 2 else 0)) * 16)
                        act.activation(rows_out[:, (m + 2) % 4, :], bank[6 + m % 2][:, 0:D], ACT.Copy).then_inc(blk.s_y, 1)
                pipeline(act, blk.tiles, step)

            expert_scalar(X2)
            for t in range(NT):
                if t % TB == 0:
                    b = t // TB
                    act.wait_ge(s_shift, b + 1)
                    act.activation(h3_sb[:, t + 1, :], x2_sb[:, t + 1, :], ACT.Identity, bias=shift[:, b:b + 1],
                                   scale=rstd[:, 3, t + 1:t + 2]).then_inc(s_norm3_act, 1)
                act.wait_ge(s_h3T, t + 1)
                if t >= 2:
                    act.wait_ge(s_logit, t - 1)
                act.activation(h3T_sb[:, t % 2, :, :], bank[t % 2][:, 0:D], ACT.Copy).then_inc(s_h3T_sb, 1)
            act.wait_ge(s_gap, 1)
            for k in range(TOPK):
                act.activation(top_w[:, k, :], gap[:, :], ACT.Sigmoid, scale=1.0 - 2.0 * k).then_inc(s_topw, 1)
            expert_scalar(X3)

        @block.tensor
        def _(pe):
            def product(dst, lhs, rhs, signal=None):
                for k, (a, c) in enumerate(zip(lhs, rhs)):
                    ins = pe.matmul(dst, a, c, start=(k == 0), stop=(k == len(lhs) - 1))
                if signal is not None:
                    ins.then_inc(signal, 1)

            def cols(a, k):
                return a[:, k * P:(k + 1) * P]

            pe.wait_ge(s_wattn, 16)
            for i in range(KD):
                product(bank[3][:, i * D:(i + 1) * D], [cols(qkv_sb[:, 0, k, :], i) for k in range(KD)],
                        [qkv_sb[:, 1, k, :] for k in range(KD)], s_qk if i == KD - 1 else None)

            def value_output_weights():
                pe.wait_ge(s_wv, 16)
                pe.wait_ge(s_wo, 16)
                for i in range(KD):
                    product(bank[4][:, i * D:(i + 1) * D], [cols(qkv_sb[:, 2, k, :], i) for k in range(KD)],
                            [wo_sb[:, k, :] for k in range(KD)], s_vo if i == KD - 1 else None)

            def transpose_xn(b):
                pe.wait_ge(s_norm[1], TB * (b + 1))
                if b == 0:
                    pe.wait_ge(s_ident, 1)
                else:
                    pe.wait_ge(s_xnT_sb, KD * b)
                for k in range(KD):
                    for i in range(TB):
                        ins = pe.transpose(bank[0][:, k * S + i * P:k * S + (i + 1) * P], cols(xn_sb[:, b * TB + i, :], k), ident[:, :])
                ins.then_inc(s_xnT, 1)

            def project_keys(b):
                xT = xnT_sb[:, b % 2]
                pe.wait_ge(s_xnT_sb, KD * (b + 1))
                if b == 0:
                    pe.wait_ge(s_qk_sb, 1)
                else:
                    pe.wait_ge(s_pT_sb, b)
                for j in range(KD):
                    product(bank[1][:, j * S:(j + 1) * S], [cols(qk_sb[:, k, :], j) for k in range(KD)],
                            [xT[:, k, :] for k in range(KD)], s_pT if j == KD - 1 else None)

            def project_values(b):
                xT = xnT_sb[:, b % 2]
                if b == 0:
                    pe.wait_ge(s_vo_sb, 1)
                else:
                    pe.wait_ge(s_vv_sb, b)
                for i in range(TB):
                    product(bank[2][:, i * D:(i + 1) * D], [cols(xT[:, k, :], i) for k in range(KD)],
                            [vo_sb[:, k, :] for k in range(KD)], s_vv if i == TB - 1 else None)

            def scores(b):
                xT, pT = xnT_sb[:, b % 2], pT_sb[:, b % 2]
                pe.wait_ge(s_pT_sb, b + 1)
                if b == 0:
                    pe.wait_ge(s_const, 2)
                if b >= 1:
                    pe.wait_ge(s_exp, TB * b)
                for i in range(TB):
                    n = (i + 1) * P
                    dst = bank[3 + i]
                    pe.matmul(dst[:, 0:n], ident_bf[:, :], causal_bf[:, S - n:S], start=True, stop=False)
                    for k in range(KD):
                        ins = pe.matmul(dst[:, 0:n], cols(pT[:, k, :], i), xT[:, k, 0:n], start=False,
                                        stop=(k == KD - 1))
                    ins.then_inc(s_score, 1)

            def transpose_probs(b):
                pe.wait_ge(s_exp, TB * (b + 1))
                if b >= 1:
                    pe.wait_ge(s_probT_sb, b)
                for n, (i, j) in enumerate(((0, 0), (1, 0), (1, 1))):
                    ins = pe.transpose(bank[5][:, n * P:(n + 1) * P], cols(prob_sb[:, b % 2, i, :], j), ident[:, :])
                ins.then_inc(s_probT, 1)

            def attend(b):
                pe.wait_ge(s_probT_sb, b + 1)
                pe.wait_ge(s_vv_sb, b + 1)
                if b >= 1:
                    pe.wait_ge(s_x1, TB * b)
                vv, pT = vv_sb[:, b % 2], probT_sb[:, b % 2]
                product(bank[6][:, 0:D], [pT[:, 0, :]], [vv[:, 0, :]])
                product(bank[6][:, D:2 * D], [pT[:, 1, :], pT[:, 2, :]], [vv[:, 0, :], vv[:, 1, :]], s_attn)

            def slot_counts(R):
                pe.wait_ge(R.s_onehot, 1)
                flat = R.onehot[:, :, :].rearrange("p e c -> p (e c)")
                pe.matmul(R.psum[:, 0:R.E * R.C], before_bf[:, :], flat, start=True, stop=True)
                pe.matmul(R.psum[:, 256:256 + R.E * R.C], ones_bf[:, :], flat, start=True, stop=True).then_inc(R.s_counts, 1)

            def slot_table(R):
                for c in range(R.C):
                    pe.wait_ge(R.s_rows, c + 1)
                    ins = pe.matmul(R.psum_table, R.at_row[:, c, :], R.at_tile[:, c, :, :].rearrange("p a j -> p (a j)"),
                                    start=(c == 0), stop=(c == R.C - 1))
                ins.then_inc(R.s_table, 1)

            def expert_tensor(blk):
                experts = blk.routing.tile_expert

                loaded = {}

                def load_expert(j):
                    return pe.value_load(experts[0:1, bass.ds(j, 1)], min_val=0, max_val=blk.first_w.shape[2] - 1)

                def rows_transpose(j, m, q, known):
                    pe.wait_ge(blk.s_in[m % 4], q * 16)
                    if known is None or known >= 2:
                        pe.wait_ge(blk.s_rowsT_sb, j - 1)
                    if blk is X3 and (known is None or known >= 4):
                        pe.wait_ge(blk.s_rest_sb, j - 3)
                    for k in range(KD):
                        ins = pe.transpose(bank[m % 2][:, k * P:(k + 1) * P], cols(rows_in[:, m % 4, :], k), ident[:, :])
                    ins.then_inc(blk.s_rowsT, 1)

                def step(i, m, q, known):
                    if known is None or known < blk.tiles:
                        loaded[2] = load_expert(i)
                    if 0 not in loaded and (known is None or known >= 2):
                        loaded[0] = load_expert(i - 2)
                    if known == 0:
                        rows_transpose(0, 0, 1, 0)
                    if known is None or known >= 2:
                        pe.wait_ge(blk.s_prod, i - 1)
                        if known is None or known >= 4:
                            pe.wait_ge(blk.s_prodT_sb, i - 3)
                            if blk is X3:
                                pe.wait_ge(blk.s_rest_sb, i - 3)
                        src, dst = prod_sb[:, m % 2], bank[4 + m % 2]
                        pe.transpose(dst[:, 0:P], src[:, 0:P], ident[:, :])
                        if blk is X2:
                            rest = dst[:, P:2 * P]
                        else:
                            rest = bank[m % 2][0:blk.width - P, D:D + P]
                            if known is None or known < blk.tiles:
                                pe.wait_ge(blk.s_rowsT_sb, i + 1)
                        pe.transpose(rest, src[:, P:blk.width], ident[:, :]).then_inc(blk.s_prodT, 1)
                    if known is None or known + 1 < blk.tiles:
                        rows_transpose(i + 1, (m + 1) % 4, q + (2 if m == 3 else 1), None if known is None else known + 1)
                    if known is None or known < blk.tiles:
                        e = loaded[2]
                        pe.wait_ge(blk.s_rowsT_sb, i + 1)
                        if known is None or known >= 2:
                            pe.wait_ge(blk.s_prod, i - 1)
                        product(bank[2 + m % 2][:, 0:blk.first_n], [rowsT[:, m % 2, k, :] for k in range(KD)],
                                [blk.first_w[:, k, bass.ds(e, 1), :] for k in range(KD)], blk.s_first)
                    if known is None or known >= 2:
                        e = loaded[0]
                        pe.wait_ge(blk.s_prodT_sb, i - 1)
                        if blk is X3:
                            pe.wait_ge(blk.s_rest_sb, i - 1)
                        if known is None or known >= 4:
                            pe.wait_ge(blk.s_y, i - 3)
                        rest = blk.width - P
                        product(bank[6 + m % 2][:, 0:D], [prodT[:, m % 2, 0, :], prodT[0:rest, m % 2, 1, :]],
                                [blk.second_w[0][:, bass.ds(e, 1), :], blk.second_w[1][:, bass.ds(e, 1), :]], blk.s_second)
                    fresh = {k - 1: v for k, v in loaded.items() if k > 0}
                    loaded.clear()
                    loaded.update(fresh)

                def turn():
                    loaded.clear()
                pipeline(pe, blk.tiles, step, turn)

            transpose_xn(0)
            pe.wait_ge(s_idsf, 1)
            pe.transpose(bank[7][:, 0:NT], ids_f[:, :], ident[0:NT, 0:NT]).then_inc(s_idsT, 1)
            value_output_weights()
            project_keys(0)
            transpose_xn(1)
            project_values(0)
            pe.wait_ge(s_const, 3)
            slot_counts(R2)
            scores(0)
            for b in range(B):
                if b + 1 < B:
                    project_keys(b + 1)
                transpose_probs(b)
                if b + 2 < B:
                    transpose_xn(b + 2)
                if b + 1 < B:
                    project_values(b + 1)
                    scores(b + 1)
                attend(b)
                if b == 0:
                    slot_table(R2)
            pe.wait_ge(s_ctx, 16)
            pe.wait_ge(R2.s_ready, 1)
            expert_tensor(X2)

            def gate(t):
                if t == 0:
                    pe.wait_ge(s_gate, 16)
                pe.wait_ge(s_h3T_sb, t + 1)
                if t >= 2:
                    pe.wait_ge(s_idx8, t - 1)
                product(bank[2 + t % 2][:, 0:E3], [h3T_sb[:, t % 2, k, :] for k in range(KD)],
                        [gate_sb[:, k, :] for k in range(KD)], s_logit)

            for t in range(NT):
                pe.wait_ge(s_norm[3] if t % TB == 0 else s_norm3_act, t // TB + 1)
                if t >= 2:
                    pe.wait_ge(s_h3T_sb, t - 1)
                for k in range(KD):
                    ins = pe.transpose(bank[t % 2][:, k * P:(k + 1) * P], cols(h3_sb[:, t, :], k), ident[:, :])
                ins.then_inc(s_h3T, 1)
                if t % (NT // 2) > 0:
                    gate(t - 1)
                if (t + 1) % (NT // 2) == 0:
                    gate(t)
            slot_counts(R3)
            slot_table(R3)
            for s in (s_w13, s_w2a, s_w2b):
                pe.wait_ge(s, 16)
            pe.wait_ge(R3.s_ready, 1)
            expert_tensor(X3)


def build(nc, args):
    decoder_layer(nc, *args)


def kernel(**inputs):
    import concourse.bacc as _bacc
    from concourse import mybir as _mybir
    from concourse.bass_utils import run_bass_kernel_spmd as _run

    a = {k: np.asarray(v) for k, v in inputs.items()}
    x = a["x"]
    T, D = x.shape[0] * x.shape[1], x.shape[2]
    KD = D // P
    ctx, qkv, wo = a["ctx_2048"], a["L0_attn_qkv"], a["L0_attn_o_proj"]
    w1, w2, w3, gate = a["L0_ffn_w1"], a["L0_ffn_w2"], a["L0_ffn_w3"], a["L0_ffn_gate_w"]
    E2, E3 = ctx.shape[0], gate.shape[0]
    laid = {
        "x": x.reshape(T, D),
        "ids": a["itok_BxS_13_99985"],
        "ctx_t": ctx.reshape(E2, D, KD, P).transpose(3, 2, 0, 1),
        "qkv_t": qkv.reshape(D, 3, KD, P).transpose(3, 1, 2, 0),
        "wo": wo.reshape(KD, P, D).transpose(1, 0, 2),
        "gamma_beta": np.stack([a["L0_attn_gamma"], a["L0_attn_beta"]]).reshape(2, KD, P).transpose(2, 0, 1),
        "gate_t": gate.reshape(E3, KD, P).transpose(2, 1, 0),
        "w13_t": np.concatenate([w1, w3], axis=1).reshape(E3, -1, KD, P).transpose(3, 2, 0, 1),
        "w2_lo_t": w2[:, :, 0:P].transpose(2, 0, 1),
        "w2_hi_t": w2[:, :, P:].transpose(2, 0, 1),
    }
    nc = _bacc.Bacc("TRN2", target_bir_lowering=False, num_devices=1)
    arrays, args = {}, []
    for name, v in laid.items():
        v = np.ascontiguousarray(v)
        arrays[f"in_{name}"] = v
        args.append(nc.dram_tensor(f"in_{name}", v.shape, _mybir.dt.from_np(v.dtype), kind="ExternalInput").ap())
    args.append(nc.dram_tensor("out_rows", [T, D], _mybir.dt.float32, kind="ExternalOutput").ap())
    build(nc, args)
    r = _run(nc, [arrays], core_ids=[0])
    return r.results[0]["out_rows"].reshape(x.shape)
```

```python
from contextlib import ExitStack

import numpy as np

import concourse.bass as bass
from concourse import mybir

F32 = mybir.dt.float32
F32R = mybir.dt.float32r
BF16 = mybir.dt.bfloat16
I32 = mybir.dt.int32
U32 = mybir.dt.uint32
ALU = mybir.AluOpType
ACT = mybir.ActivationFunctionType
AX = mybir.AxisListType

P = 128
EPS = 1e-5
MASKED = -1e30
ROUND = 1.5 * 2.0 ** 23


def decoder_layer(nc, x, ids, ctx_t, qkv_t, wo, gamma_beta, gate_t, w13_t, w2_lo_t, w2_hi_t, out):
    T, D = x.shape
    KD = D // P
    NT = T // P
    B = ids.shape[0]
    TB = NT // B
    S = T // B
    E2 = ctx_t.shape[2]
    VOCAB = 12500
    PER_EXPERT = VOCAB // E2
    E3 = gate_t.shape[2]
    TOPK = 2
    F3 = w13_t.shape[3] // 2
    F3R = F3 - P
    HALVES = 2
    BH = B // HALVES
    NT2H = T // P // HALVES + E2 - 1
    NT2 = HALVES * NT2H
    NT3 = TOPK * T // P + E3 - 1
    POOL_ROWS = 4
    LOOP = 8
    FIRST = 6
    assert KD == 2 and TB == 2 and B == 4 and D == 256 and 4 * F3R == P and P < F3 <= 2 * P

    with ExitStack() as stack:
        def sb(name, shape, dt=F32):
            return stack.enter_context(nc.sbuf_tensor(name, shape, dt))

        def sem(name):
            return stack.enter_context(nc.semaphore(name))

        h2_dram = [nc.dram_tensor(f"h2_rows{h}", [T // HALVES, D], F32).ap() for h in range(HALVES)]
        y2_dram = nc.dram_tensor("y2_rows", [T + NT2 * P, D], F32).ap()
        h3_dram = nc.dram_tensor("h3_rows", [T, D], F32).ap()
        y3_dram = nc.dram_tensor("y3_rows", [TOPK * T + NT3 * P, D], F32).ap()

        bank = [stack.enter_context(nc.psum_tensor(f"bank{i}", [P, 512], F32)) for i in range(8)]

        ident = sb("ident", [P, P])
        ident_bf = sb("ident_bf", [P, P], BF16)
        causal_bf = sb("causal_bf", [P, S], BF16)
        before_bf = sb("before_bf", [P, P], BF16)
        ones_bf = sb("ones_bf", [P, P], BF16)
        iota_slot = sb("iota_slot", [P, P])
        iota_bf = sb("iota_bf", [P, P], BF16)
        iota_part = sb("iota_part", [P, 1])
        iota_col = sb("iota_col", [P, TOPK * NT])
        pow_half = sb("pow_half", [P, TB])

        qkv_sb = sb("qkv_sb", [P, 3, KD, D])
        wo_sb = sb("wo_sb", [P, KD, D])
        gb_sb = sb("gb_sb", [P, 2, KD])
        qk_sb = sb("qk_sb", [P, KD, D])
        vo_sb = sb("vo_sb", [P, KD, D])
        ctx_sb = sb("ctx_sb", [P, KD, E2, D])
        gate_sb = sb("gate_sb", [P, KD, E3])
        w13_sb = sb("w13_sb", [P, KD, E3, 2 * F3])
        w2a_sb = sb("w2a_sb", [P, E3, D])
        w2r_sb = sb("w2r_sb", [P, E3, D], F32R)

        x_sb = sb("x_sb", [P, NT, D])
        h1_sb = sb("h1_sb", [P, NT, D])
        xn_sb = sb("xn_sb", [P, NT, D])
        xh_sb = sb("xh_sb", [P, NT, D])
        x1_sb = sb("x1_sb", [P, NT, D])
        h2_sb = xn_sb
        x2_sb = x_sb
        h3_sb = h1_sb
        y2_sb = xh_sb
        y3_sb = sb("y3_sb", [P, TOPK, NT, D])
        w2_rest = y3_sb[:, :, :, :].rearrange("p k t d -> p (k t) d")[:, 0:E3, :]
        out_sb = x1_sb

        NORMS = 4
        stats = sb("stats", [P, NORMS, NT, 6])
        meanvar = sb("meanvar", [P, NORMS, NT, 2])
        vareps = sb("vareps", [P, NORMS, NT])
        rstd = sb("rstd", [P, NORMS, NT])
        shift = sb("shift", [P, B])

        xnT_sb = sb("xnT_sb", [P, 2, KD, S])
        pT_sb = sb("pT_sb", [P, 2, KD, S])
        vv_sb = sb("vv_sb", [P, 2, TB, D])
        prob_sb = sb("prob_sb", [P, 2, TB, S])
        probT_sb = sb("probT_sb", [P, 2, 3, P])
        negmax = sb("negmax", [P, NT])
        rowsum = sb("rowsum", [P, NT])
        rowinv = sb("rowinv", [P, NT])

        class Routing:
            def __init__(self, tag, E, C, tiles):
                self.tag, self.E, self.C, self.tiles = tag, E, C, tiles
                self.expert = sb(f"{tag}_expert", [P, C])
                self.onehot = sb(f"{tag}_onehot", [P, E, C], BF16)
                self.goes_on = sb(f"{tag}_goes_on", [P, E, C])
                self.cum = sb(f"{tag}_cum", [P, E, C])
                self.rank = sb(f"{tag}_rank", [P, E, C])
                self.ntile_x = sb(f"{tag}_ntile_x", [P, E])
                self.ntile = sb(f"{tag}_ntile", [P, E])
                self.carry = sb(f"{tag}_carry", [P, E])
                self.end = sb(f"{tag}_end", [P, E])
                self.start = sb(f"{tag}_start", [P, E])
                self.slot = sb(f"{tag}_slot", [P, C])
                self.tile_x = sb(f"{tag}_tile_x", [P, C])
                self.tile_of = sb(f"{tag}_tile_of", [P, C])
                self.row_of = sb(f"{tag}_row_of", [P, C])
                self.at_row = sb(f"{tag}_at_row", [P, C, P], BF16)
                self.at_tile = sb(f"{tag}_at_tile", [P, C, 3, tiles], BF16)
                self.table = sb(f"{tag}_table", [P, 3, tiles])
                self.spare = sb(f"{tag}_spare", [P, tiles])
                self.unused = sb(f"{tag}_unused", [P, tiles])
                self.dest_f = sb(f"{tag}_dest_f", [P, tiles])
                self.dest = sb(f"{tag}_dest", [P, tiles], I32)
                self.src = sb(f"{tag}_src", [P, tiles], I32)
                self.past = sb(f"{tag}_past", [P, tiles, E])
                self.tile_f = sb(f"{tag}_tile_f", [P, tiles])
                self.tile_expert = sb(f"{tag}_tile_expert", [P, tiles], I32)
                self.s_onehot = sem(f"{tag}_s_onehot")
                self.s_counts = sem(f"{tag}_s_counts")
                self.s_step = sem(f"{tag}_s_step")
                self.s_init = sem(f"{tag}_s_init")
                self.s_slots = sem(f"{tag}_s_slots")
                self.s_rows = sem(f"{tag}_s_rows")
                self.s_rows_pool = sem(f"{tag}_s_rows_pool")
                self.s_payload = sem(f"{tag}_s_payload")
                self.s_experts = sem(f"{tag}_s_experts")
                self.s_table = sem(f"{tag}_s_table")
                self.s_ready = sem(f"{tag}_s_ready")

        R2 = Routing("r2", HALVES * E2, NT, NT2)
        half_first = sb("half_first", [P, NT])
        half_offset = sb("half_offset", [P, HALVES * E2])
        half_counted = sb("half_counted", [P, NT2])
        half_last = sb("half_last", [P, NT2])
        ntile_offset = sb("ntile_offset", [P, HALVES * E2])
        R3 = Routing("r3", E3, TOPK * NT, NT3)
        R2.psum, R2.psum_table = bank[7], bank[7][:, 64:64 + 3 * NT2]
        R2.rows, R3.rows = T // HALVES, T
        R3.psum, R3.psum_table = bank[4], bank[5][:, 0:3 * NT3]
        ids_sb = sb("ids_sb", [NT, P], I32)
        ids_f = sb("ids_f", [NT, P])
        top_val = sb("top_val", [P, NT, 8])
        top_idx = sb("top_idx", [P, NT, 8], U32)
        gap = sb("gap", [P, NT])
        top_w = sb("top_w", [P, TOPK, NT])
        h3T_sb = sb("h3T_sb", [P, 2, KD, P])

        rows_in = sb("rows_in", [P, 4, D])
        rowsT = sb("rowsT", [P, 2, KD, P])
        silu_sb = sb("silu_sb", [P, 2, D])
        prod_sb = sb("prod_sb", [P, 2, D])
        prodT = sb("prodT", [P, 2, 2, P])
        rest_sb = sb("rest_sb", [P, 2, 4, F3R], F32R)
        restT = sb("restT", [P, 2, P], F32R)
        rows_out = sb("rows_out", [P, 4, D])

        s_ids = sem("s_ids")
        s_x = [sem(f"s_x_in{b}") for b in range(B)]
        s_wattn = sem("s_wattn")
        s_wv = sem("s_wv")
        s_wo = sem("s_wo")
        s_gb = sem("s_gb")
        s_ctx = sem("s_ctx")
        s_gate = sem("s_gate")
        s_w13 = sem("s_w13")
        s_w2a = sem("s_w2a")
        s_w2_rest = sem("s_w2_rest")
        s_w2_high = sem("s_w2_high")
        s_w2_low = sem("s_w2_low")
        s_fill = sem("s_fill")
        s_ident = sem("s_ident")
        s_const = sem("s_const")
        s_qk = sem("s_qk")
        s_vo = sem("s_vo")
        s_qk_sb = sem("s_qk_sb")
        s_vo_sb = sem("s_vo_sb")
        s_stat = [sem(f"s_stat{n}") for n in range(NORMS)]
        s_mv = [sem(f"s_mv{n}") for n in range(NORMS)]
        s_var = [sem(f"s_var{n}") for n in range(NORMS)]
        s_rstd = [sem(f"s_rstd{n}") for n in range(NORMS)]
        s_norm = [sem(f"s_norm{n}") for n in range(NORMS)]
        s_xh = sem("s_xh")
        s_xnT = sem("s_xnT")
        s_xnT_sb = sem("s_xnT_sb")
        s_pT = sem("s_pT")
        s_pT_sb = sem("s_pT_sb")
        s_vv = sem("s_vv")
        s_vv_sb = sem("s_vv_sb")
        s_score = sem("s_score")
        s_max = sem("s_max")
        s_exp = sem("s_exp")
        s_probT = sem("s_probT")
        s_probT_sb = sem("s_probT_sb")
        s_inv = sem("s_inv")
        s_attn = sem("s_attn")
        s_x1 = sem("s_x1")
        s_h2_out = [sem(f"s_h2_out{b}") for b in range(B)]
        s_y2_in = [sem(f"s_y2_in{b}") for b in range(B)]
        s_x2 = sem("s_x2")
        s_x2_last = sem("s_x2_last")
        s_shift = sem("s_shift")
        s_norm3_act = sem("s_norm3_act")
        s_h3_out = sem("s_h3_out")
        s_h3T = sem("s_h3T")
        s_h3T_sb = sem("s_h3T_sb")
        s_logit = sem("s_logit")
        s_max8 = sem("s_max8")
        s_idx8 = sem("s_idx8")
        s_gap = sem("s_gap")
        s_topw = sem("s_topw")
        s_idsf = sem("s_idsf")
        s_idsT = sem("s_idsT")
        s_y3_in = [[sem(f"s_y3_in{k}_{b}") for b in range(B)] for k in range(TOPK)]
        s_mix = sem("s_mix")
        s_sum = sem("s_sum")
        s_out = sem("s_out")

        class ExpertBlock:
            def __init__(self, tag, routing, first_w, first_n, width, second_w, src, dst):
                self.routing, self.tiles = routing, routing.tiles
                self.first_w, self.first_n, self.width = first_w, first_n, width
                self.second_w, self.src, self.dst = second_w, src, dst
                self.s_in = [sem(f"{tag}_in{m}") for m in range(4)]
                self.s_rowsT = sem(f"{tag}_rowsT")
                self.s_rowsT_sb = sem(f"{tag}_rowsT_sb")
                self.s_first = sem(f"{tag}_first")
                self.s_silu = sem(f"{tag}_silu")
                self.s_prod = sem(f"{tag}_prod")
                self.s_high = sem(f"{tag}_high")
                self.s_low = sem(f"{tag}_low")
                self.s_prodT = sem(f"{tag}_prodT")
                self.s_prodT_sb = sem(f"{tag}_prodT_sb")
                self.s_rest_sb = sem(f"{tag}_rest_sb")
                self.s_second = sem(f"{tag}_second")
                self.s_y = sem(f"{tag}_y")
                self.s_done = [sem(f"{tag}_done{m}") for m in range(4)]

            def scattered(self, eng, tiles):
                for m in range(4):
                    eng.wait_ge(self.s_done[m], 16 * len(range(m, tiles, 4)))

        X2 = ExpertBlock("x2", R2, ctx_sb, D, D, [ctx_sb[:, k] for k in range(KD)], h2_dram, y2_dram)
        X3 = ExpertBlock("x3", R3, w13_sb, 2 * F3, F3, [w2a_sb], [h3_dram], y3_dram)

        def pipeline(eng, tiles, step, turn=lambda: None):
            def at(i):
                step(i, i % 4, i // 4, i)
            turns = (tiles - 1 - FIRST) // LOOP
            if turns < 2:
                turns = 0
            for i in range(FIRST):
                at(i)
            if turns:
                with nc.Fori(0, turns, engines=(eng.engine,), hint_back_edge=True) as n:
                    turn()
                    for u in range(FIRST, FIRST + LOOP):
                        step(n * LOOP + u, u % 4, n * (LOOP // 4) + u // 4, None)
            turn()
            for i in range(FIRST + LOOP * turns, tiles + 2):
                at(i)

        block = stack.enter_context(nc.Block())

        @block.sync
        def _(sp):
            rows = x.rearrange("(c p) d -> p c d", p=P)
            for b in range(B):
                sp.dma_start(x_sb[:, b * TB:(b + 1) * TB, :], rows[:, b * TB:(b + 1) * TB, :]).then_inc(s_x[b], 16)
            sp.dma_start(gate_sb[:, :, :], gate_t).then_inc(s_gate, 16)
            sp.dma_start(ctx_sb[:, :, :, :], ctx_t).then_inc(s_ctx, 16)
            sp.dma_start(w13_sb[:, :, :, :], w13_t).then_inc(s_w13, 16)
            sp.dma_start(w2a_sb[:, :, :], w2_lo_t).then_inc(s_w2a, 16)
            for g in range(4):
                sp.dma_start(w2_rest[g * F3R:(g + 1) * F3R, :, :], w2_hi_t).then_inc(s_w2_rest, 16)
            h3_rows = h3_dram.rearrange("(c p) d -> p c d", p=P)
            for b in range(B):
                sp.wait_ge(s_norm[2], TB * (b + 1))
                h2_rows = h2_dram[b // BH].rearrange("(c p) d -> p c d", p=P)
                sp.dma_start(h2_rows[:, b % BH * TB:(b % BH + 1) * TB, :], h2_sb[:, b * TB:(b + 1) * TB, :]).then_inc(s_h2_out[b], 16)
            y2_rows = y2_dram[0:T, :].rearrange("(c p) d -> p c d", p=P)
            for b in range(B):
                if b % BH == 0:
                    X2.scattered(sp, NT2H * (b // BH + 1))
                sp.dma_start(y2_sb[:, b * TB:(b + 1) * TB, :], y2_rows[:, b * TB:(b + 1) * TB, :]).then_inc(s_y2_in[b], 16)
            for b in range(B):
                sp.wait_ge(s_norm[3], b + 1)
                sp.wait_ge(s_norm3_act, b + 1)
                sp.dma_start(h3_rows[:, b * TB:(b + 1) * TB, :], h3_sb[:, b * TB:(b + 1) * TB, :]).then_inc(s_h3_out, 16)
            X3.scattered(sp, NT3)
            y3_rows = y3_dram[0:TOPK * T, :].rearrange("(k c p) d -> p k c d", k=TOPK, p=P)
            for b in range(B):
                for k in range(TOPK):
                    sp.dma_start(y3_sb[:, k, b * TB:(b + 1) * TB, :], y3_rows[:, k, b * TB:(b + 1) * TB, :]).then_inc(s_y3_in[k][b], 16)
            out_rows = out.rearrange("(c p) d -> p c d", p=P)
            for b in range(B):
                sp.wait_ge(s_sum, TB * (b + 1))
                sp.dma_start(out_rows[:, b * TB:(b + 1) * TB, :], out_sb[:, b * TB:(b + 1) * TB, :]).then_inc(s_out, 16)
            sp.wait_ge(s_out, 16 * B)

        @block.gpsimd
        def _(pool):
            pool.memset(ident[:, :], 0.0).then_inc(s_fill, 1)
            pool.memset(pow_half[:, :], -0.5).then_inc(s_fill, 1)
            pool.wait_ge(s_fill, 1)
            pool.affine_select(out=ident[:, :], in_=ident[:, :], compare_op=ALU.not_equal, fill=1.0, base=0,
                               pattern=[[-1, P]], channel_multiplier=1).then_inc(s_ident, 1)
            pool.memset(causal_bf[:, :], 0.0).then_inc(s_fill, 1)
            pool.memset(before_bf[:, :], 1.0).then_inc(s_fill, 1)
            pool.memset(ones_bf[:, :], 1.0).then_inc(s_fill, 1)
            pool.wait_ge(s_ident, 1)
            pool.tensor_copy(ident_bf[:, :], ident[:, :]).then_inc(s_const, 1)
            pool.wait_ge(s_fill, 5)
            pool.affine_select(out=causal_bf[:, :], in_=causal_bf[:, :], compare_op=ALU.is_ge, fill=MASKED, base=S - P,
                               pattern=[[-1, S]], channel_multiplier=1).then_inc(s_const, 1)
            pool.affine_select(out=before_bf[:, :], in_=before_bf[:, :], compare_op=ALU.is_gt, fill=0.0, base=0,
                               pattern=[[1, P]], channel_multiplier=-1).then_inc(s_const, 1)
            pool.iota(iota_slot[:, :], pattern=[[1, P]], base=0, channel_multiplier=0,
                      allow_small_or_imprecise_dtypes=True).then_inc(s_const, 1)
            pool.iota(iota_part[:, :], pattern=[[0, 1]], base=0, channel_multiplier=1,
                      allow_small_or_imprecise_dtypes=True).then_inc(s_const, 1)
            pool.iota(iota_col[:, :], pattern=[[1, TOPK * NT]], base=0, channel_multiplier=0,
                      allow_small_or_imprecise_dtypes=True).then_inc(s_const, 1)

            pool.iota(iota_bf[:, :], pattern=[[1, P]], base=0, channel_multiplier=0,
                      allow_small_or_imprecise_dtypes=True).then_inc(s_const, 1)
            for R in (R2, R3):
                pool.iota(R.spare[:, :], pattern=[[P, R.tiles]], base=R.C * P, channel_multiplier=1,
                          allow_small_or_imprecise_dtypes=True).then_inc(s_const, 1)

            def inverse_root(n, b):
                pool.wait_ge(s_var[n], b + 1)
                pool.tensor_tensor(rstd[:, n, b * TB:(b + 1) * TB], vareps[:, n, b * TB:(b + 1) * TB], pow_half[:, :],
                                   ALU.pow).then_inc(s_rstd[n], 1)

            def residual(b):
                pool.wait_ge(s_norm[0], TB * (b + 1))
                pool.tensor_tensor(xh_sb[:, b * TB:(b + 1) * TB, :], x_sb[:, b * TB:(b + 1) * TB, :],
                                   h1_sb[:, b * TB:(b + 1) * TB, :], ALU.add).then_inc(s_xh, 1)

            def half_ready(j):
                if j % NT2H == 0:
                    for b in range(BH):
                        pool.wait_ge(s_h2_out[j // NT2H * BH + b], 16)

            def route_by_slot(blk, start, ready=None, between=lambda j: None):
                def gather(j):
                    if ready is not None:
                        ready(j)
                    if j >= 4:
                        pool.wait_ge(blk.s_rowsT, j - 3)
                    pool.indirect_dma_start(
                        out=rows_in[:, j % 4, :], out_offset=None, in_=blk.src[j * len(blk.src) // blk.tiles],
                        in_offset=bass.IndirectOffsetOnAxis(ap=blk.routing.src[:, j:j + 1].bitcast(U32), axis=0),
                    ).then_inc(blk.s_in[j % 4], 16)

                def scatter(j):
                    pool.wait_ge(blk.s_y, j + 1)
                    pool.indirect_dma_start(
                        out=blk.dst, in_=rows_out[:, j % 4, :], in_offset=None,
                        out_offset=bass.IndirectOffsetOnAxis(ap=blk.routing.dest[:, j:j + 1].bitcast(U32), axis=0),
                    ).then_inc(blk.s_done[j % 4], 16)

                if start is not None:
                    for j in start:
                        gather(j)
                    return
                LAG = 3
                for j in range(blk.tiles + LAG):
                    if j + 4 < blk.tiles:
                        gather(j + 4)
                    if j >= LAG:
                        scatter(j - LAG)
                    between(j - LAG)

            inverse_root(0, 0)
            inverse_root(1, 0)
            inverse_root(0, 1)
            inverse_root(1, 1)
            inverse_root(0, 2)
            inverse_root(1, 2)
            inverse_root(0, 3)
            inverse_root(1, 3)
            residual(0)
            residual(1)
            residual(2)
            residual(3)
            for b in range(B):
                if b == B - 1:
                    pool.wait_ge(R2.s_ready, 1)
                    route_by_slot(X2, range(0, 2), half_ready)
                if b >= 1:
                    inverse_root(2, b - 1)
            route_by_slot(X2, range(2, 4), half_ready)
            inverse_root(2, B - 1)
            def first_half_roots(j):
                if j in (NT2 - 3, NT2 - 1):
                    inverse_root(3, 0 if j == NT2 - 3 else 1)
            route_by_slot(X2, None, half_ready, first_half_roots)
            last = slice((B - 1) * TB, B * TB)
            pool.wait_ge(s_y2_in[B - 1], 16)
            pool.wait_ge(s_rstd[3], BH)
            pool.tensor_tensor(x2_sb[:, last, :], x1_sb[:, last, :], y2_sb[:, last, :], ALU.add).then_inc(s_x2_last, 1)
            for b in range(BH, B):
                inverse_root(3, b)
            pool.wait_ge(s_rstd[3], B)
            pool.wait_ge(R3.s_slots, 2)
            for c in range(R3.C - POOL_ROWS, R3.C):
                if c > R3.C - POOL_ROWS:
                    pool.wait_ge(R3.s_rows_pool, c - (R3.C - POOL_ROWS))
                pool.tensor_scalar(R3.at_row[:, c, :], iota_bf[:, :], R3.row_of[:, c:c + 1], None,
                                   ALU.is_equal).then_inc(R3.s_rows_pool, 1)
            pool.wait_ge(R3.s_rows_pool, POOL_ROWS)
            pool.wait_ge(s_h3_out, 16 * B)
            pool.wait_ge(R3.s_ready, 1)
            route_by_slot(X3, range(4))
            route_by_slot(X3, None)

        @block.vector
        def _(dve):
            for R in (R2, R3):
                dve.memset(R.carry[:, :], 1.0).then_inc(R.s_init, 1)
                dve.memset(R.goes_on[:, :, :], 1.0).then_inc(R.s_init, 1)
            dve.memset(half_first[:, :], 0.0).then_inc(R2.s_init, 1)
            dve.memset(half_offset[:, :], 0.0).then_inc(R2.s_init, 1)
            dve.memset(half_counted[:, :], 0.0).then_inc(R2.s_init, 1)
            dve.memset(half_last[:, :], float(E2 - 1)).then_inc(R2.s_init, 1)
            for R in (R2, R3):
                dve.wait_ge(R.s_init, 2)
                dve.memset(R.goes_on[:, :, 0:1], 0.0).then_inc(R.s_init, 1)
            dve.wait_ge(R2.s_init, 6)
            dve.memset(R2.carry[:, E2:E2 + 1], 0.0).then_inc(R2.s_init, 1)
            dve.memset(half_first[:, NT // 2:NT], float(E2)).then_inc(R2.s_init, 1)
            dve.memset(half_offset[:, E2:E2 + 1], float(NT2H)).then_inc(R2.s_init, 1)
            dve.memset(half_counted[:, NT2H:NT2], float(E2)).then_inc(R2.s_init, 1)
            dve.memset(half_last[:, NT2H:NT2], float(2 * E2 - 1)).then_inc(R2.s_init, 1)

            def moments(n, src, b):
                ts = range(b * TB, (b + 1) * TB)
                for t in ts:
                    dve.bn_stats(stats[:, n, t, :], src[:, t, :]).then_inc(s_stat[n], 1)
                for t in ts:
                    dve.wait_ge(s_stat[n], t + 1)
                    dve.bn_aggr(meanvar[:, n, t, :], stats[:, n, t, :]).then_inc(s_mv[n], 1)
                dve.wait_ge(s_mv[n], TB * (b + 1))
                dve.tensor_scalar(vareps[:, n, b * TB:(b + 1) * TB], meanvar[:, n, b * TB:(b + 1) * TB, 1], EPS, None,
                                  ALU.add).then_inc(s_var[n], 1)

            def normalise(n, dst, src, b):
                dve.wait_ge(s_rstd[n], b + 1)
                for t in range(b * TB, (b + 1) * TB):
                    dve.tensor_scalar(dst[:, t, :], src[:, t, :], meanvar[:, n, t, 0:1], rstd[:, n, t:t + 1],
                                      ALU.subtract, ALU.mult).then_inc(s_norm[n], 1)

            def norm_a(b):
                dve.wait_ge(s_x[b], 16)
                moments(0, x_sb, b)

            def norm_b(b):
                normalise(0, h1_sb, x_sb, b)
                dve.wait_ge(s_norm[0], TB * (b + 1))
                moments(1, h1_sb, b)

            def norm_c(b):
                normalise(1, xn_sb, h1_sb, b)

            def row_max(b):
                for i in range(TB):
                    t = b * TB + i
                    dve.wait_ge(s_score, t + 1)
                    dve.tensor_reduce(negmax[:, t:t + 1], bank[3 + i][:, 0:(i + 1) * P], AX.X, ALU.max,
                                      negate=True).then_inc(s_max, 1)

            def prob_transposed(b):
                dve.wait_ge(s_probT, b + 1)
                if b >= 2:
                    dve.wait_ge(s_attn, b - 1)
                dve.tensor_copy(probT_sb[:, b % 2, :, :], bank[5][:, 0:3 * P]).then_inc(s_probT_sb, 1)

            def row_inverse(b):
                dve.wait_ge(s_exp, TB * (b + 1))
                dve.reciprocal(rowinv[:, b * TB:(b + 1) * TB], rowsum[:, b * TB:(b + 1) * TB]).then_inc(s_inv, 1)

            def attention_out(b):
                dve.wait_ge(s_attn, b + 1)
                dve.wait_ge(s_inv, b + 1)
                dve.wait_ge(s_xh, b + 1)
                for i in range(TB):
                    t = b * TB + i
                    dve.scalar_tensor_tensor(out=x1_sb[:, t, :], in0=bank[6][:, i * D:(i + 1) * D],
                                             scalar=rowinv[:, t:t + 1], in1=xh_sb[:, t, :], op0=ALU.mult,
                                             op1=ALU.add).then_inc(s_x1, 1)

            def moments_2(b):
                dve.wait_ge(s_x1, TB * (b + 1))
                moments(2, x1_sb, b)

            def token_experts():
                dve.wait_ge(s_idsT, 1)
                dve.wait_ge(R2.s_init, 12)
                for e in range(1, E2):
                    if e > 1:
                        dve.wait_ge(R2.s_step, e - 1)
                    dve.scalar_tensor_tensor(out=R2.expert[:, :], in0=bank[7][:, 0:NT], scalar=float(e * PER_EXPERT),
                                             in1=half_first[:, :] if e == 1 else R2.expert[:, :],
                                             op0=ALU.is_ge, op1=ALU.add).then_inc(R2.s_step, 1)
                dve.wait_ge(R2.s_step, E2 - 1)

            class Steps:
                def __init__(self, R, done):
                    self.R, self.n = R, done

                def step(self, ins):
                    self.n += 1
                    ins.then_inc(self.R.s_step, 1)

                def join(self):
                    dve.wait_ge(self.R.s_step, self.n)

            def slot_onehot(R):
                E, C = R.E, R.C
                dve.tensor_tensor(R.onehot[:, :, :], iota_slot[:, 0:E].rearrange("p (e o) -> p e o", o=1).to_broadcast([P, E, C]),
                                  R.expert[:, :].rearrange("p (o c) -> p o c", o=1).to_broadcast([P, E, C]),
                                  ALU.is_equal).then_inc(R.s_onehot, 1)

            def slot_ranks(R, done):
                own = Steps(R, done)
                step, join = own.step, own.join
                E, C, NTL = R.E, R.C, R.tiles
                dve.wait_ge(R.s_counts, 1)
                in_tile = R.psum[:, 0:E * C]
                totals = R.psum[:, 256:256 + E * C]
                flat = lambda a: a[:, :, :].rearrange("p e c -> p (e c)")
                step(dve.tensor_tensor_scan(flat(R.cum), flat(R.goes_on), totals, 0.0, ALU.mult, ALU.add))
                join()
                step(dve.tensor_tensor(flat(R.rank), flat(R.cum), totals, ALU.subtract))
                step(dve.tensor_scalar(R.ntile_x[:, :], R.cum[:, :, C - 1], 1.0 / P, (P - 1) / (2.0 * P), ALU.mult, ALU.add))
                join()
                step(dve.tensor_tensor(flat(R.rank), flat(R.rank), in_tile, ALU.add))
                step(dve.tensor_scalar(R.ntile[:, :], R.ntile_x[:, :], ROUND, -ROUND, ALU.add, ALU.add))
                join()
                widths = R.ntile
                if R is R2:
                    widths = ntile_offset
                    step(dve.tensor_tensor(widths[:, :], R.ntile[:, :], half_offset[:, :], ALU.add))
                    join()
                step(dve.tensor_tensor_scan(R.end[:, :], R.carry[:, :], widths[:, :], 0.0, ALU.mult, ALU.add))
                join()
                step(dve.tensor_tensor(R.start[:, :], R.end[:, :], R.ntile[:, :], ALU.subtract))
                join()
                step(dve.scalar_tensor_tensor(out=R.rank[:, :, :],
                                              in0=R.start[:, :].rearrange("p (e o) -> p e o", o=1).to_broadcast([P, E, C]),
                                              scalar=float(P), in1=R.rank[:, :, :], op0=ALU.mult, op1=ALU.add))
                join()
                step(dve.tensor_tensor(R.rank[:, :, :], R.rank[:, :, :], R.onehot[:, :, :], ALU.mult))
                join()
                step(dve.tensor_reduce(R.slot[:, :], R.rank[:, :, :].rearrange("p e c -> p c e"), AX.X, ALU.add))
                join()
                step(dve.tensor_scalar(R.tile_x[:, :], R.slot[:, :], 1.0 / P, -(P - 1) / (2.0 * P), ALU.mult, ALU.add))
                return own.n

            def tile_experts(R, done):
                own = Steps(R, done)
                step, join = own.step, own.join
                E, NTL = R.E, R.tiles
                step(dve.tensor_tensor(R.past[:, :, :],
                                       iota_slot[:, 0:NTL].rearrange("p (j o) -> p j o", o=1).to_broadcast([P, NTL, E]),
                                       R.end[:, :].rearrange("p (o e) -> p o e", o=1).to_broadcast([P, NTL, E]), ALU.is_ge))
                join()
                step(dve.tensor_reduce(R.tile_f[:, :], R.past[:, :, :], AX.X, ALU.add))
                join()
                if R is R2:
                    step(dve.tensor_tensor(R.tile_f[:, :], R.tile_f[:, :], half_last[:, :], ALU.min))
                    join()
                    dve.tensor_tensor(R.tile_expert[:, :], R.tile_f[:, :], half_counted[:, :], ALU.subtract).then_inc(R.s_experts, 1)
                else:
                    dve.tensor_scalar(R.tile_expert[:, :], R.tile_f[:, :], float(E - 1), None, ALU.min).then_inc(R.s_experts, 1)

            def slot_rows(R, done):
                own = Steps(R, done)
                step, join = own.step, own.join
                C, NTL = R.C, R.tiles
                join()
                step(dve.tensor_scalar(R.tile_of[:, :], R.tile_x[:, :], ROUND, -ROUND, ALU.add, ALU.add))
                join()
                dve.tensor_tensor(R.at_tile[:, :, 2, :],
                                       iota_slot[:, 0:NTL].rearrange("p (o j) -> p o j", o=1).to_broadcast([P, C, NTL]),
                                       R.tile_of[:, :].rearrange("p (c o) -> p c o", o=1).to_broadcast([P, C, NTL]),
                                       ALU.is_equal).then_inc(R.s_slots, 1)
                dve.scalar_tensor_tensor(out=R.row_of[:, :], in0=R.tile_of[:, :], scalar=float(-P), in1=R.slot[:, :],
                                              op0=ALU.mult, op1=ALU.add).then_inc(R.s_slots, 1)
                dve.wait_ge(R.s_slots, 2)
                if R is R2:
                    dve.tensor_scalar(R.at_tile[:, :, 0, :], R.at_tile[:, :, 2, :], iota_part[:, 0:1], None,
                                      ALU.mult).then_inc(R.s_payload, 1)
                dve.tensor_tensor(R.at_tile[:, :, 1, :], R.at_tile[:, :, 2, :],
                                  iota_col[:, 0:C].rearrange("p (c o) -> p c o", o=1).to_broadcast([P, C, NTL]),
                                  ALU.mult).then_inc(R.s_payload, 1)
                for c in range(C if R is R2 else C - POOL_ROWS):
                    dve.tensor_scalar(R.at_row[:, c, :], iota_bf[:, :], R.row_of[:, c:c + 1], None,
                                      ALU.is_equal).then_inc(R.s_rows, 1)
                return own.n

            def slot_tables(R, done):
                own = Steps(R, done)
                step, join = own.step, own.join
                dve.wait_ge(R.s_table, 1)
                step(dve.tensor_copy(R.table[:, :, :], R.psum_table))
                join()
                step(dve.scalar_tensor_tensor(out=R.dest_f[:, :], in0=R.table[:, 1, :], scalar=float(P),
                                              in1=R.table[:, 0, :], op0=ALU.mult, op1=ALU.add))
                step(dve.scalar_tensor_tensor(out=R.unused[:, :], in0=R.table[:, 2, :], scalar=0.0, in1=R.spare[:, :],
                                              op0=ALU.is_equal, op1=ALU.mult))
                join()
                step(dve.tensor_tensor(R.dest[:, :], R.dest_f[:, :], R.unused[:, :], ALU.add))
                join()
                dve.tensor_scalar(R.src[:, :], R.dest[:, :], R.rows - 1, None, ALU.bitwise_and).then_inc(R.s_ready, 1)
                return own.n

            def expert_vector(blk, after=lambda i: None, between=lambda i: None):
                factor0 = blk.first_n - blk.width

                def step(i, m, q, known):
                    def rows_transposed(j, mj):
                        dve.wait_ge(blk.s_rowsT, j + 1)
                        if known is None or known >= 1:
                            dve.wait_ge(blk.s_first, j - 1)
                        dve.tensor_copy(rowsT[:, mj % 2, :, :], bank[mj % 2][:, 0:D]).then_inc(blk.s_rowsT_sb, 1)

                    if known == 0:
                        dve.wait_ge(blk.s_rowsT, 1)
                        dve.tensor_copy(rowsT[:, 0, :, :], bank[0][:, 0:D]).then_inc(blk.s_rowsT_sb, 1)
                    if known is None or known + 1 < blk.tiles:
                        rows_transposed(i + 1, m + 1)
                    if blk is X3 and (known is None or 2 <= known):
                        dve.wait_ge(blk.s_prodT, i - 1)
                        if known is None or known >= 4:
                            dve.wait_ge(blk.s_second, i - 3)
                        dve.tensor_copy(restT[:, m % 2, :], bank[m % 2][:, D:D + P]).then_inc(blk.s_rest_sb, 1)
                    between(known)
                    if known is None or known < blk.tiles:
                        dve.wait_ge(blk.s_silu, i + 1)
                        if known is None or known >= 2:
                            dve.wait_ge(blk.s_prodT, i - 1)
                        dve.tensor_tensor(prod_sb[:, m % 2, 0:blk.width], silu_sb[:, m % 2, 0:blk.width],
                                          bank[2 + m % 2][:, factor0:factor0 + blk.width], ALU.mult).then_inc(blk.s_prod, 1)
                        if blk is X3:
                            last = prod_sb[:, m % 2, P:F3].rearrange("p (o f) -> p o f", o=1).to_broadcast([P, 2, F3R])
                            halves = rest_sb[:, m % 2, :, :].rearrange("p (r h) f -> p r h f", h=2)
                            high, low = halves[:, :, 0, :], halves[:, :, 1, :]
                            dve.wait_ge(blk.s_prod, i + 1)
                            dve.tensor_copy(high, last).then_inc(blk.s_high, 1)
                            dve.wait_ge(blk.s_high, i + 1)
                            dve.tensor_tensor(low, last, high.bitcast(F32),
                                              ALU.subtract).then_inc(blk.s_low, 1)
                    after(known)
                pipeline(dve, blk.tiles, step)

            norm_a(0)
            norm_b(0)
            norm_a(1)
            norm_c(0)
            norm_b(1)
            dve.wait_ge(s_ids, 16)
            dve.tensor_copy(ids_f[:, :], ids_sb[:, :]).then_inc(s_idsf, 1)
            norm_a(2)
            norm_c(1)
            token_experts()
            dve.wait_ge(s_const, 9)
            slot_onehot(R2)
            norm_b(2)
            norm_a(B - 1)
            for b in range(B):
                row_max(b)
                if b >= 1:
                    attention_out(b - 1)
                    if b < B - 1:
                        moments_2(b - 1)
                if b + 2 < B:
                    norm_c(b + 2)
                if b == B - 1:
                    moments_2(b - 1)
                else:
                    prob_transposed(b)
                row_inverse(b)
                if b == 0:
                    norm_b(B - 1)
                    n = slot_ranks(R2, E2 - 1)
                if b == 1:
                    n = slot_rows(R2, n)
                if 1 <= b < B - 1:
                    normalise(2, h2_sb, x1_sb, b - 1)
                if b == 2:
                    tile_experts(R2, slot_tables(R2, n))
            attention_out(B - 1)

            def second_residual(b):
                if b < B - 1:
                    dve.wait_ge(s_y2_in[b], 16)
                    dve.tensor_tensor(x2_sb[:, b * TB:(b + 1) * TB, :], x1_sb[:, b * TB:(b + 1) * TB, :],
                                      y2_sb[:, b * TB:(b + 1) * TB, :], ALU.add).then_inc(s_x2, 1)
                    dve.wait_ge(s_x2, b + 1)
                else:
                    dve.wait_ge(s_x2_last, 1)
                moments(3, x2_sb, b)

            def second_norm(b):
                t = b * TB
                dve.wait_ge(s_rstd[3], b + 1)
                dve.scalar_tensor_tensor(out=shift[:, b:b + 1], in0=meanvar[:, 3, t + 1, 0:1], scalar=-1.0,
                                         in1=rstd[:, 3, t + 1:t + 2], op0=ALU.mult, op1=ALU.mult).then_inc(s_shift, 1)
                dve.tensor_scalar(h3_sb[:, t, :], x2_sb[:, t, :], meanvar[:, 3, t, 0:1], rstd[:, 3, t:t + 1],
                                  ALU.subtract, ALU.mult).then_inc(s_norm[3], 1)

            def best_two(t):
                dve.wait_ge(s_logit, t + 1)
                lg = bank[2 + t % 2][:, 0:E3]
                dve.max(top_val[:, t, :], lg).then_inc(s_max8, 1)
                dve.wait_ge(s_max8, t + 1)
                dve.max_index(top_idx[:, t, :], top_val[:, t, :], lg).then_inc(s_idx8, 1)

            def first_half(i):
                n = i - (NT2 - 2)
                if 0 <= n < BH:
                    second_residual(n)
                if BH <= n < 2 * BH:
                    second_norm(n - BH)

            def last_moments(i):
                if i == 0:
                    normalise(2, h2_sb, x1_sb, B - 2)
                    moments_2(B - 1)
                if i == 1:
                    normalise(2, h2_sb, x1_sb, B - 1)

            def after(i):
                if 2 <= i < 2 + E3:
                    dve.wait_ge(s_w2_high, i - 1)
                    low = w2r_sb[2 * F3R:P, i - 2, :]
                    dve.tensor_tensor(low, w2_rest[2 * F3R:P, i - 2, :], low.bitcast(F32), ALU.subtract).then_inc(s_w2_low, 1)
                first_half(i)
            expert_vector(X2, after, last_moments)
            for t in range(NT // 2):
                best_two(t)
            for b in range(BH, B):
                second_residual(b)
            for b in range(BH, B):
                second_norm(b)
            for t in range(NT // 2, NT):
                best_two(t)
            dve.wait_ge(s_idx8, NT)
            dve.tensor_copy(R3.expert[:, :].rearrange("p (k t) -> p t k", k=TOPK), top_idx[:, :, 0:TOPK]).then_inc(R3.s_step, 1)
            dve.tensor_tensor(gap[:, :], top_val[:, :, 0], top_val[:, :, 1], ALU.subtract).then_inc(s_gap, 1)
            dve.wait_ge(R3.s_init, 3)
            dve.wait_ge(R3.s_step, 1)
            slot_onehot(R3)
            tile_experts(R3, slot_tables(R3, slot_rows(R3, slot_ranks(R3, 1))))
            expert_vector(X3)

            for b in range(B):
                ts = range(b * TB, (b + 1) * TB)
                dve.wait_ge(s_y3_in[0][b], 16)
                if b == 0:
                    dve.wait_ge(s_topw, TOPK)
                for t in ts:
                    dve.scalar_tensor_tensor(out=out_sb[:, t, :], in0=y3_sb[:, 0, t, :], scalar=top_w[:, 0, t:t + 1],
                                             in1=x2_sb[:, t, :], op0=ALU.mult, op1=ALU.add).then_inc(s_mix, 1)
                dve.wait_ge(s_y3_in[1][b], 16)
                for t in ts:
                    dve.wait_ge(s_mix, t + 1)
                    dve.scalar_tensor_tensor(out=out_sb[:, t, :], in0=y3_sb[:, 1, t, :], scalar=top_w[:, 1, t:t + 1],
                                             in1=out_sb[:, t, :], op0=ALU.mult, op1=ALU.add).then_inc(s_sum, 1)

        @block.scalar
        def _(act):
            act.dma_start(qkv_sb[:, 0:2, :, :], qkv_t[:, 0:2, :, :]).then_inc(s_wattn, 16)
            act.dma_start(ids_sb[:, :], ids.rearrange("b (c p) -> (b c) p", p=P)).then_inc(s_ids, 16)
            act.dma_start(gb_sb[:, :, :], gamma_beta).then_inc(s_gb, 16)
            act.dma_start(qkv_sb[:, 2, :, :], qkv_t[:, 2, :, :]).then_inc(s_wv, 16)
            act.dma_start(wo_sb[:, :, :], wo).then_inc(s_wo, 16)
            act.wait_ge(s_qk, 1)
            act.activation(qk_sb[:, :, :], bank[3][:, :], ACT.Copy).then_inc(s_qk_sb, 1)

            def xn_transposed(b):
                act.wait_ge(s_xnT, b + 1)
                if b == 0:
                    act.wait_ge(s_gb, 16)
                if b >= 2:
                    act.wait_ge(s_score, TB * (b - 1))
                for k in range(KD):
                    act.activation(xnT_sb[:, b % 2, k, :], bank[0][:, k * S:(k + 1) * S], ACT.Identity,
                                   bias=gb_sb[:, 1, k:k + 1], scale=gb_sb[:, 0, k:k + 1]).then_inc(s_xnT_sb, 1)

            def projected_keys(b):
                act.wait_ge(s_pT, b + 1)
                if b >= 2:
                    act.wait_ge(s_score, TB * (b - 1))
                act.activation(pT_sb[:, b % 2, :, :], bank[1][:, :], ACT.Copy, scale=float(D) ** -0.5).then_inc(s_pT_sb, 1)

            def projected_values(b):
                act.wait_ge(s_vv, b + 1)
                if b >= 2:
                    act.wait_ge(s_attn, b - 1)
                act.activation(vv_sb[:, b % 2, :, :], bank[2][:, :], ACT.Copy).then_inc(s_vv_sb, 1)

            def exponentials(b):
                for i in range(TB):
                    t = b * TB + i
                    act.wait_ge(s_max, t + 1)
                    if b >= 2 and i == 0:
                        act.wait_ge(s_probT, b - 1)
                    act.activation(prob_sb[:, b % 2, i, 0:(i + 1) * P], bank[3 + i][:, 0:(i + 1) * P],
                                   ACT.Exp, bias=negmax[:, t:t + 1], accum_out=rowsum[:, t:t + 1]).then_inc(s_exp, 1)

            xn_transposed(0)
            projected_keys(0)
            act.wait_ge(s_vo, 1)
            act.activation(vo_sb[:, :, :], bank[4][:, :], ACT.Copy).then_inc(s_vo_sb, 1)
            xn_transposed(1)
            projected_values(0)
            for b in range(B):
                exponentials(b)
                if b + 1 < B:
                    projected_keys(b + 1)
                    if b + 2 < B:
                        xn_transposed(b + 2)
                    projected_values(b + 1)
            act.wait_ge(s_probT, B)
            act.wait_ge(s_attn, B - 2)
            act.activation(probT_sb[:, (B - 1) % 2, :, :], bank[5][:, 0:3 * P], ACT.Copy).then_inc(s_probT_sb, 1)

            def expert_scalar(blk, after=lambda i: None):
                def step(i, m, q, known):
                    def product_transposed(i, m, known):
                        act.wait_ge(blk.s_prodT, i - 1)
                        if known is None or known >= 4:
                            act.wait_ge(blk.s_second, i - 3)
                        n = D if blk is X2 else P
                        act.activation(prodT[:, m % 2, 0:n // P, :], bank[4 + m % 2][:, 0:n], ACT.Copy).then_inc(blk.s_prodT_sb, 1)

                    if known is None or 2 <= known <= blk.tiles:
                        product_transposed(i, m, known)
                    if known == blk.tiles:
                        product_transposed(i + 1, m + 1, known + 1)
                    if known is None or known < blk.tiles:
                        act.wait_ge(blk.s_first, i + 1)
                        if known is None or known >= 2:
                            act.wait_ge(blk.s_prod, i - 1)
                        act.activation(silu_sb[:, m % 2, 0:blk.width], bank[2 + m % 2][:, 0:blk.width], ACT.Silu).then_inc(blk.s_silu, 1)
                    if known is None or known >= 2:
                        act.wait_ge(blk.s_second, i - 1)
                        if known is None or known >= 6:
                            act.wait_ge(blk.s_done[(m + 2) % 4], (q - (1 if m < 2 else 0)) * 16)
                        act.activation(rows_out[:, (m + 2) % 4, :], bank[6 + m % 2][:, 0:D], ACT.Copy).then_inc(blk.s_y, 1)
                    after(known)
                pipeline(act, blk.tiles, step)

            def split_rest(i):
                if i == 1:
                    act.wait_ge(s_w2_rest, 16 * 4)
                if 1 <= i <= E3:
                    act.activation(w2r_sb[:, i - 1, :], w2_rest[:, i - 1, :], ACT.Copy).then_inc(s_w2_high, 1)
            expert_scalar(X2, split_rest)
            for t in range(NT):
                if t % TB == 0:
                    b = t // TB
                    act.wait_ge(s_shift, b + 1)
                    act.activation(h3_sb[:, t + 1, :], x2_sb[:, t + 1, :], ACT.Identity, bias=shift[:, b:b + 1],
                                   scale=rstd[:, 3, t + 1:t + 2]).then_inc(s_norm3_act, 1)
                act.wait_ge(s_h3T, t + 1)
                if t >= 2:
                    act.wait_ge(s_logit, t - 1)
                act.activation(h3T_sb[:, t % 2, :, :], bank[t % 2][:, 0:D], ACT.Copy).then_inc(s_h3T_sb, 1)
            act.wait_ge(s_gap, 1)
            for k in range(TOPK):
                act.activation(top_w[:, k, :], gap[:, :], ACT.Sigmoid, scale=1.0 - 2.0 * k).then_inc(s_topw, 1)
            act.wait_ge(R3.s_slots, 2)
            act.activation(R3.at_tile[:, :, 0, :], R3.at_tile[:, :, 2, :], ACT.Copy, scale=iota_part[:, 0:1]).then_inc(R3.s_payload, 1)
            expert_scalar(X3)

        @block.tensor
        def _(pe):
            def product(dst, lhs, rhs, signal=None):
                for k, (a, c) in enumerate(zip(lhs, rhs)):
                    ins = pe.matmul(dst, a, c, start=(k == 0), stop=(k == len(lhs) - 1))
                if signal is not None:
                    ins.then_inc(signal, 1)

            def cols(a, k):
                return a[:, k * P:(k + 1) * P]

            def stay_warm(dst, n):
                for _ in range(n):
                    pe.matmul(dst[:, 0:S], ident_bf[:, :], causal_bf[:, :], start=True, stop=True)

            pe.wait_ge(s_const, 2)
            stay_warm(bank[5], 10)
            pe.wait_ge(s_wattn, 16)
            for i in range(KD):
                product(bank[3][:, i * D:(i + 1) * D], [cols(qkv_sb[:, 0, k, :], i) for k in range(KD)],
                        [qkv_sb[:, 1, k, :] for k in range(KD)], s_qk if i == KD - 1 else None)

            def value_output_weights():
                pe.wait_ge(s_wv, 16)
                pe.wait_ge(s_wo, 16)
                for i in range(KD):
                    product(bank[4][:, i * D:(i + 1) * D], [cols(qkv_sb[:, 2, k, :], i) for k in range(KD)],
                            [wo_sb[:, k, :] for k in range(KD)], s_vo if i == KD - 1 else None)

            def transpose_xn(b):
                pe.wait_ge(s_norm[1], TB * (b + 1))
                if b == 0:
                    pe.wait_ge(s_ident, 1)
                else:
                    pe.wait_ge(s_xnT_sb, KD * b)
                for k in range(KD):
                    for i in range(TB):
                        ins = pe.transpose(bank[0][:, k * S + i * P:k * S + (i + 1) * P], cols(xn_sb[:, b * TB + i, :], k), ident[:, :])
                ins.then_inc(s_xnT, 1)

            def project_keys(b):
                xT = xnT_sb[:, b % 2]
                pe.wait_ge(s_xnT_sb, KD * (b + 1))
                if b == 0:
                    pe.wait_ge(s_qk_sb, 1)
                else:
                    pe.wait_ge(s_pT_sb, b)
                for j in range(KD):
                    product(bank[1][:, j * S:(j + 1) * S], [cols(qk_sb[:, k, :], j) for k in range(KD)],
                            [xT[:, k, :] for k in range(KD)], s_pT if j == KD - 1 else None)

            def project_values(b):
                xT = xnT_sb[:, b % 2]
                if b == 0:
                    pe.wait_ge(s_vo_sb, 1)
                else:
                    pe.wait_ge(s_vv_sb, b)
                for i in range(TB):
                    product(bank[2][:, i * D:(i + 1) * D], [cols(xT[:, k, :], i) for k in range(KD)],
                            [vo_sb[:, k, :] for k in range(KD)], s_vv if i == TB - 1 else None)

            def scores(b):
                xT, pT = xnT_sb[:, b % 2], pT_sb[:, b % 2]
                pe.wait_ge(s_pT_sb, b + 1)
                if b == 0:
                    pe.wait_ge(s_const, 2)
                if b >= 1:
                    pe.wait_ge(s_exp, TB * b)
                for i in range(TB):
                    n = (i + 1) * P
                    dst = bank[3 + i]
                    pe.matmul(dst[:, 0:n], ident_bf[:, :], causal_bf[:, S - n:S], start=True, stop=False)
                    for k in range(KD):
                        ins = pe.matmul(dst[:, 0:n], cols(pT[:, k, :], i), xT[:, k, 0:n], start=False,
                                        stop=(k == KD - 1))
                    ins.then_inc(s_score, 1)

            def transpose_probs(b):
                pe.wait_ge(s_exp, TB * (b + 1))
                if b >= 1:
                    pe.wait_ge(s_probT_sb, b)
                for n, (i, j) in enumerate(((0, 0), (1, 0), (1, 1))):
                    ins = pe.transpose(bank[5][:, n * P:(n + 1) * P], cols(prob_sb[:, b % 2, i, :], j), ident[:, :])
                ins.then_inc(s_probT, 1)

            def attend(b):
                pe.wait_ge(s_probT_sb, b + 1)
                pe.wait_ge(s_vv_sb, b + 1)
                if b >= 1:
                    pe.wait_ge(s_x1, TB * b)
                vv, pT = vv_sb[:, b % 2], probT_sb[:, b % 2]
                product(bank[6][:, 0:D], [pT[:, 0, :]], [vv[:, 0, :]])
                product(bank[6][:, D:2 * D], [pT[:, 1, :], pT[:, 2, :]], [vv[:, 0, :], vv[:, 1, :]], s_attn)

            def slot_counts(R):
                pe.wait_ge(R.s_onehot, 1)
                flat = R.onehot[:, :, :].rearrange("p e c -> p (e c)")
                pe.matmul(R.psum[:, 0:R.E * R.C], before_bf[:, :], flat, start=True, stop=True)
                pe.matmul(R.psum[:, 256:256 + R.E * R.C], ones_bf[:, :], flat, start=True, stop=True).then_inc(R.s_counts, 1)

            def slot_table(R):
                pe.wait_ge(R.s_payload, 2)
                for c in range(R.C):
                    own = R.C if R is R2 else R.C - POOL_ROWS
                    if c < own:
                        pe.wait_ge(R.s_rows, c + 1)
                    else:
                        pe.wait_ge(R.s_rows_pool, c - own + 1)
                    if R is R3:
                        stay_warm(bank[6], 1)
                    ins = pe.matmul(R.psum_table, R.at_row[:, c, :], R.at_tile[:, c, :, :].rearrange("p a j -> p (a j)"),
                                    start=(c == 0), stop=(c == R.C - 1))
                ins.then_inc(R.s_table, 1)

            def expert_tensor(blk):
                experts = blk.routing.tile_expert

                loaded = {}

                def load_expert(j):
                    return pe.value_load(experts[0:1, bass.ds(j, 1)], min_val=0, max_val=blk.first_w.shape[2] - 1)

                def rows_transpose(j, m, q, known):
                    pe.wait_ge(blk.s_in[m % 4], q * 16)
                    if known is None or known >= 2:
                        pe.wait_ge(blk.s_rowsT_sb, j - 1)
                    if blk is X3 and (known is None or known >= 4):
                        pe.wait_ge(blk.s_rest_sb, j - 3)
                    for k in range(KD):
                        ins = pe.transpose(bank[m % 2][:, k * P:(k + 1) * P], cols(rows_in[:, m % 4, :], k), ident[:, :])
                    ins.then_inc(blk.s_rowsT, 1)

                def product_transpose(i, m, known):
                    pe.wait_ge(blk.s_low if blk is X3 else blk.s_prod, i - 1)
                    if known is None or known >= 4:
                        pe.wait_ge(blk.s_prodT_sb, i - 3)
                        if blk is X3:
                            pe.wait_ge(blk.s_rest_sb, i - 3)
                    src, dst = prod_sb[:, m % 2], bank[4 + m % 2]
                    pe.transpose(dst[:, 0:P], src[:, 0:P], ident[:, :])
                    if blk is X2:
                        rest, last = dst[:, P:2 * P], src[:, P:D]
                    else:
                        rest = bank[m % 2][:, D:D + P]
                        last = rest_sb[:, m % 2, :, :].rearrange("p g f -> p (g f)").bitcast(F32)
                        if known is None or known < blk.tiles:
                            pe.wait_ge(blk.s_rowsT_sb, i + 1)
                    pe.transpose(rest, last, ident[:, :]).then_inc(blk.s_prodT, 1)

                def step(i, m, q, known):
                    if 2 not in loaded and (known is None or known < blk.tiles):
                        loaded[2] = load_expert(i)
                    if 0 not in loaded and (known is None or known >= 2):
                        loaded[0] = load_expert(i - 2)
                    if known == 0:
                        rows_transpose(0, 0, 1, 0)
                    if known is None or 2 <= known <= blk.tiles:
                        product_transpose(i, m, known)
                    if known == blk.tiles:
                        product_transpose(i + 1, m + 1, known + 1)
                    late = 0 if blk is X3 else None
                    if known is None or (known != late and known < blk.tiles - 1):
                        rows_transpose(i + 1, (m + 1) % 4, q + (2 if m == 3 else 1), None if known is None else known + 1)
                    if known is None or known < blk.tiles:
                        e = loaded[2]
                        pe.wait_ge(blk.s_rowsT_sb, i + 1)
                        if known is None or known >= 2:
                            pe.wait_ge(blk.s_prod, i - 1)
                        product(bank[2 + m % 2][:, 0:blk.first_n], [rowsT[:, m % 2, k, :] for k in range(KD)],
                                [blk.first_w[:, k, bass.ds(e, 1), :] for k in range(KD)], blk.s_first)
                    if known is not None and known == late:
                        rows_transpose(1, 1, 1, 1)
                    if known is None or known + 1 < blk.tiles:
                        loaded[3] = load_expert(i + 1)
                    if known is None or known >= 2:
                        e = loaded[0]
                        pe.wait_ge(blk.s_prodT_sb, i - 1)
                        if blk is X3:
                            pe.wait_ge(blk.s_rest_sb, i - 1)
                        if known is None or known >= 4:
                            pe.wait_ge(blk.s_y, i - 3)
                        lhs = [prodT[:, m % 2, k, :] for k in range(len(blk.second_w))]
                        rhs = [w[:, bass.ds(e, 1), :] for w in blk.second_w]
                        if blk is X3:
                            lhs.append(restT[:, m % 2, :])
                            rhs.append(w2r_sb[:, bass.ds(e, 1), :])
                        product(bank[6 + m % 2][:, 0:D], lhs, rhs, blk.s_second)
                    fresh = {k - 1: v for k, v in loaded.items() if k > 0}
                    loaded.clear()
                    loaded.update(fresh)

                def turn():
                    loaded.clear()
                pipeline(pe, blk.tiles, step, turn)

            transpose_xn(0)
            project_keys(0)
            value_output_weights()
            pe.wait_ge(s_idsf, 1)
            pe.transpose(bank[7][:, 0:NT], ids_f[:, :], ident[0:NT, 0:NT]).then_inc(s_idsT, 1)
            transpose_xn(1)
            project_values(0)
            pe.wait_ge(s_const, 3)
            slot_counts(R2)
            scores(0)
            for b in range(B):
                if b + 1 < B:
                    project_keys(b + 1)
                transpose_probs(b)
                if b + 2 < B:
                    transpose_xn(b + 2)
                if b + 1 < B:
                    project_values(b + 1)
                    scores(b + 1)
                attend(b)
                if b == 1:
                    slot_table(R2)
            pe.wait_ge(s_ctx, 16)
            pe.wait_ge(R2.s_experts, 1)
            expert_tensor(X2)

            def gate(t):
                if t == 0:
                    pe.wait_ge(s_gate, 16)
                pe.wait_ge(s_h3T_sb, t + 1)
                if t >= 2:
                    pe.wait_ge(s_idx8, t - 1)
                product(bank[2 + t % 2][:, 0:E3], [h3T_sb[:, t % 2, k, :] for k in range(KD)],
                        [gate_sb[:, k, :] for k in range(KD)], s_logit)

            for t in range(NT):
                if t == NT // 2:
                    stay_warm(bank[4], 42)
                pe.wait_ge(s_norm[3] if t % TB == 0 else s_norm3_act, t // TB + 1)
                if t >= 2:
                    pe.wait_ge(s_h3T_sb, t - 1)
                for k in range(KD):
                    ins = pe.transpose(bank[t % 2][:, k * P:(k + 1) * P], cols(h3_sb[:, t, :], k), ident[:, :])
                ins.then_inc(s_h3T, 1)
                stay_warm(bank[4], 4 if t < NT // 2 else 2)
                if t % (NT // 2) > 0:
                    gate(t - 1)
                if (t + 1) % (NT // 2) == 0:
                    gate(t)
            slot_counts(R3)
            stay_warm(bank[6], 34)
            slot_table(R3)
            stay_warm(bank[6], 34)
            for s in (s_w13, s_w2a):
                pe.wait_ge(s, 16)
            pe.wait_ge(s_w2_low, E3)
            pe.wait_ge(R3.s_experts, 1)
            expert_tensor(X3)


def build(nc, args):
    decoder_layer(nc, *args)


def kernel(**inputs):
    import concourse.bacc as _bacc
    from concourse import mybir as _mybir
    from concourse.bass_utils import run_bass_kernel_spmd as _run

    a = {k: np.asarray(v) for k, v in inputs.items()}
    x = a["x"]
    T, D = x.shape[0] * x.shape[1], x.shape[2]
    KD = D // P
    ctx, qkv, wo = a["ctx_2048"], a["L0_attn_qkv"], a["L0_attn_o_proj"]
    w1, w2, w3, gate = a["L0_ffn_w1"], a["L0_ffn_w2"], a["L0_ffn_w3"], a["L0_ffn_gate_w"]
    E2, E3 = ctx.shape[0], gate.shape[0]
    laid = {
        "x": x.reshape(T, D),
        "ids": a["itok_BxS_13_99985"],
        "ctx_t": ctx.reshape(E2, D, KD, P).transpose(3, 2, 0, 1),
        "qkv_t": qkv.reshape(D, 3, KD, P).transpose(3, 1, 2, 0),
        "wo": wo.reshape(KD, P, D).transpose(1, 0, 2),
        "gamma_beta": np.stack([a["L0_attn_gamma"], a["L0_attn_beta"]]).reshape(2, KD, P).transpose(2, 0, 1),
        "gate_t": gate.reshape(E3, KD, P).transpose(2, 1, 0),
        "w13_t": np.concatenate([w1, w3], axis=1).reshape(E3, -1, KD, P).transpose(3, 2, 0, 1),
        "w2_lo_t": w2[:, :, 0:P].transpose(2, 0, 1),
        "w2_hi_t": w2[:, :, P:].transpose(2, 0, 1),
    }
    nc = _bacc.Bacc("TRN2", target_bir_lowering=False, num_devices=1)
    arrays, args = {}, []
    for name, v in laid.items():
        v = np.ascontiguousarray(v)
        arrays[f"in_{name}"] = v
        args.append(nc.dram_tensor(f"in_{name}", v.shape, _mybir.dt.from_np(v.dtype), kind="ExternalInput").ap())
    args.append(nc.dram_tensor("out_rows", [T, D], _mybir.dt.float32, kind="ExternalOutput").ap())
    build(nc, args)
    r = _run(nc, [arrays], core_ids=[0])
    return r.results[0]["out_rows"].reshape(x.shape)
```
